# Optimizing a Trainium2 kernel written in Bass

```python
import numpy as np
import jax
import jax.numpy as jnp

def _softmax(x, axis=-1):
    return jax.nn.softmax(x, axis=axis)

def _gelu(x):
    return jax.nn.gelu(x, approximate=True)

def _silu(x):
    return jax.nn.silu(x)

def _sigmoid(x):
    return jax.nn.sigmoid(x)

def _layernorm(x, axis=-1, eps=1e-05):
    m = jnp.mean(x, axis=axis, keepdims=True)
    v = jnp.var(x, axis=axis, keepdims=True)
    return (x - m) / jnp.sqrt(v + eps)

def _scatter_add(tgt, idx, src, axis=0):
    return tgt.at[idx].add(src)

def _segment_sum(src, seg, n):
    return jax.ops.segment_sum(src, seg, n)
kernel_name = 'mk_prb_d1_jaxref_r8_9a9192'

def setup_inputs(seed: int=0):
    np.random.seed(seed)
    _w = jnp.asarray

    def _L0_attn_setup():
        import jax, jax.numpy as jnp
        import numpy as np
        import math
        HID_DIM = 128
        NUM_HEADS = 8
        QK_DIM = HID_DIM // 8
        key = jax.random.key(seed)
        ks = jax.random.split(key, 7)
        B, M, C = (4, 256, HID_DIM)
        gain = math.sqrt(2.0)

        def xavier(k, fan_in, fan_out):
            std = gain * math.sqrt(2.0 / (fan_in + fan_out))
            a = math.sqrt(3.0) * std
            return jax.random.uniform(k, (fan_out, fan_in), jnp.float32, -a, a)
        x = jax.random.normal(ks[0], (B, M, C), jnp.float32)
        Wq = xavier(ks[1], C, QK_DIM)
        Wk = xavier(ks[2], C, QK_DIM)
        Wv = xavier(ks[3], C, C)
        bq = jnp.zeros((QK_DIM,), jnp.float32)
        bk = jnp.zeros((QK_DIM,), jnp.float32)
        bv = jnp.zeros((C,), jnp.float32)
        gamma = jnp.zeros((1,), jnp.float32)
        return {'x': x, 'Wq': Wq, 'bq': bq, 'Wk': Wk, 'bk': bk, 'Wv': Wv, 'bv': bv, 'gamma': gamma}
    _L0_attn_in = _L0_attn_setup()

    def _L0_ffn_setup():
        import math
        import jax, jax.numpy as jnp
        import numpy as np
        B, S, H = (4, 512, 128)
        FFN = 512
        E = 16
        N_ZERO, N_COPY, N_CONST = (1, 1, 2)
        MLP_START = N_ZERO + N_COPY + N_CONST
        E_MLP = E - MLP_START
        TOP_K = 2
        CAP_FACTOR = 1.0
        EPS = 1e-05

        def _rmsnorm(x, w, eps):
            return x * jax.lax.rsqrt(jnp.mean(x * x, axis=-1, keepdims=True) + eps) * w
        key = jax.random.key(seed)
        ks = jax.random.split(key, 6)
        std = jnp.float32(0.02)
        return {'x': jax.random.normal(ks[0], (B, S, H), jnp.float32), 'norm_weight': jnp.ones((H,), jnp.float32), 'router_weight': jax.random.normal(ks[1], (E, H), jnp.float32) * std, 'router_bias': jnp.zeros((E,), jnp.float32), 'fc1_weight': jax.random.normal(ks[2], (E_MLP, FFN, H), jnp.float32) * std, 'fc1_bias': jnp.zeros((E_MLP, FFN), jnp.float32), 'fc2_weight': jax.random.normal(ks[3], (E_MLP, H, FFN), jnp.float32) * std, 'fc2_bias': jnp.zeros((E_MLP, H), jnp.float32), 'constant_vectors': jax.random.normal(ks[4], (N_CONST, H), jnp.float32) * std}
    _L0_ffn_in = _L0_ffn_setup()
    _d = {'L0_attn_x': _L0_attn_in['x'], 'L0_attn_Wq': _L0_attn_in['Wq'], 'L0_attn_bq': _L0_attn_in['bq'], 'L0_attn_Wk': _L0_attn_in['Wk'], 'L0_attn_bk': _L0_attn_in['bk'], 'L0_attn_Wv': _L0_attn_in['Wv'], 'L0_attn_bv': _L0_attn_in['bv'], 'L0_attn_gamma': _L0_attn_in['gamma'], 'L0_ffn_norm_weight': _L0_ffn_in['norm_weight'], 'L0_ffn_router_weight': _L0_ffn_in['router_weight'], 'L0_ffn_router_bias': _L0_ffn_in['router_bias'], 'L0_ffn_fc1_weight': _L0_ffn_in['fc1_weight'], 'L0_ffn_fc1_bias': _L0_ffn_in['fc1_bias'], 'L0_ffn_fc2_weight': _L0_ffn_in['fc2_weight'], 'L0_ffn_fc2_bias': _L0_ffn_in['fc2_bias'], 'L0_ffn_constant_vectors': _L0_ffn_in['constant_vectors']}
    _x0 = _d['L0_attn_x']
    _d['L0_attn_x'] = jax.random.normal(jax.random.fold_in(jax.random.key(seed), 1), (8, 1024, 128), dtype=_x0.dtype)
    del _x0
    return _d

def reference(L0_attn_x, L0_attn_Wq, L0_attn_bq, L0_attn_Wk, L0_attn_bk, L0_attn_Wv, L0_attn_bv, L0_attn_gamma, L0_ffn_norm_weight, L0_ffn_router_weight, L0_ffn_router_bias, L0_ffn_fc1_weight, L0_ffn_fc1_bias, L0_ffn_fc2_weight, L0_ffn_fc2_bias, L0_ffn_constant_vectors):

    def _L0_attn_ref(x, Wq, bq, Wk, bk, Wv, bv, gamma):
        import jax, jax.numpy as jnp
        import numpy as np
        import math
        HID_DIM = 128
        NUM_HEADS = 8
        QK_DIM = HID_DIM // 8
        B, M, C = x.shape
        H = NUM_HEADS
        dqk = QK_DIM // H
        dv = C // H
        q = (x @ Wq.T + bq).reshape(B, M, H, dqk)
        k = (x @ Wk.T + bk).reshape(B, M, H, dqk)
        v = (x @ Wv.T + bv).reshape(B, M, H, dv)
        scores = jnp.einsum('bmhd,bnhd->bhmn', q, k) / math.sqrt(dqk)
        scores = jnp.where(scores >= 0, scores, 0.2 * scores)
        beta = jax.nn.softmax(scores, axis=-1)
        out = jnp.einsum('bhmn,bnhd->bmhd', beta, v).reshape(B, M, C)
        return gamma * out + x

    def _L0_ffn_ref(x, norm_weight, router_weight, router_bias, fc1_weight, fc1_bias, fc2_weight, fc2_bias, constant_vectors):
        import math
        import jax, jax.numpy as jnp
        import numpy as np
        B, S, H = (4, 512, 128)
        FFN = 512
        E = 16
        N_ZERO, N_COPY, N_CONST = (1, 1, 2)
        MLP_START = N_ZERO + N_COPY + N_CONST
        E_MLP = E - MLP_START
        TOP_K = 2
        CAP_FACTOR = 1.0
        EPS = 1e-05

        def _rmsnorm(x, w, eps):
            return x * jax.lax.rsqrt(jnp.mean(x * x, axis=-1, keepdims=True) + eps) * w
        Bsz, Sl, Hd = x.shape
        N = Bsz * Sl
        CAP = int(math.ceil(CAP_FACTOR * N * TOP_K / E))
        x_flat = x.reshape(N, Hd)
        xn = _rmsnorm(x_flat, norm_weight, EPS)
        logits = xn @ router_weight.T + router_bias
        probs = jax.nn.softmax(logits, axis=-1)
        gate_vals, expert_idx = jax.lax.top_k(probs, TOP_K)
        e_flat = expert_idx.reshape(-1)
        g_flat = gate_vals.reshape(-1)
        oh = jax.nn.one_hot(e_flat, E, dtype=jnp.int32)
        pos = jnp.sum(jnp.cumsum(oh, axis=0) * oh, axis=-1) - 1
        keep = pos < CAP
        slot = jnp.clip(pos, 0, CAP - 1)
        tok = jnp.repeat(jnp.arange(N), TOP_K)
        contrib = xn[tok] * keep[:, None].astype(x.dtype)
        dispatch = jnp.zeros((E, CAP, Hd), x.dtype).at[e_flat, slot].add(contrib)
        out_zero = jnp.zeros((N_ZERO, CAP, Hd), x.dtype)
        out_copy = dispatch[N_ZERO:N_ZERO + N_COPY]
        out_const = jnp.broadcast_to(constant_vectors[:, None, :], (N_CONST, CAP, Hd))
        dm = dispatch[MLP_START:]
        h = jnp.einsum('ech,efh->ecf', dm, fc1_weight) + fc1_bias[:, None, :]
        h = jax.nn.gelu(h, approximate=False)
        out_mlp = jnp.einsum('ecf,ehf->ech', h, fc2_weight) + fc2_bias[:, None, :]
        expert_out = jnp.concatenate([out_zero, out_copy, out_const, out_mlp], axis=0)
        gathered = expert_out[e_flat, slot]
        w = g_flat * keep.astype(g_flat.dtype)
        combined = (gathered * w[:, None]).reshape(N, TOP_K, Hd).sum(axis=1)
        gate_sums = w.reshape(N, TOP_K).sum(axis=1, keepdims=True)
        out = combined / jnp.where(gate_sums > 0, gate_sums, 1.0)
        return out.reshape(Bsz, Sl, Hd)
    x = L0_attn_x
    xn = _layernorm(x, axis=-1)
    x = x + _L0_attn_ref(xn, L0_attn_Wq, L0_attn_bq, L0_attn_Wk, L0_attn_bk, L0_attn_Wv, L0_attn_bv, L0_attn_gamma) + _L0_ffn_ref(xn, L0_ffn_norm_weight, L0_ffn_router_weight, L0_ffn_router_bias, L0_ffn_fc1_weight, L0_ffn_fc1_bias, L0_ffn_fc2_weight, L0_ffn_fc2_bias, L0_ffn_constant_vectors)
    return x

_drawn_inputs = setup_inputs


def setup_inputs(seed=0):
    import zlib

    import numpy as np

    out = dict(_drawn_inputs(seed))
    spreads = {'L0_attn_bq': (0.0, 0.1),
     'L0_attn_bk': (0.0, 0.1),
     'L0_attn_bv': (0.0, 0.1),
     'L0_ffn_norm_weight': (1.0, 0.2),
     'L0_ffn_router_bias': (0.0, 0.1),
     'L0_ffn_fc1_bias': (0.0, 0.8),
     'L0_ffn_fc2_bias': (0.0, 0.276)}
    factors = {'L0_ffn_fc1_weight': 3.545, 'L0_ffn_fc2_weight': 3.194, 'L0_ffn_constant_vectors': 21.822}
    for name, (base, spread) in spreads.items():
        noise = np.random.default_rng([zlib.crc32(name.encode()), seed]).standard_normal(out[name].shape)
        drawn = base * np.exp(spread * noise) if base else spread * noise
        out[name] = jnp.asarray(drawn.astype(out[name].dtype))
    for name, factor in factors.items():
        out[name] = (out[name] * factor).astype(out[name].dtype)
    return out
```

```python
from contextlib import ExitStack

import concourse.bass as bass
from concourse import mybir

F32 = mybir.dt.float32
BF16 = mybir.dt.bfloat16
I32 = mybir.dt.int32
ALU = mybir.AluOpType
ACT = mybir.ActivationFunctionType
AX = mybir.AxisListType

P = 128
B, M, C = 8, 1024, 128
T = B * M
NT = T // P
TB = M // P
H, DV, DQ = 8, 16, 2
HG = 4
NHG = H // HG
GT = 4
GW = GT * P
HALF = 512
QP = H * DQ
KROW = 64
PROWS = KROW + 3 * QP
NPROD = 3 * 3 * DQ
NROW = NPROD + 1
DIRS = 16
E, E_MLP, FFN = 16, 12, 512
FC = FFN // P
MLP0 = E - E_MLP
CAP = T * 2 // E
SLOTS = E_MLP * CAP
ST = CAP // P
SKIP = float(1 << 20)
EPS = 1e-5
SLOPE = 0.2

C_ID, C_TRI, C_KDIR, C_PDIR, C_RDIR, C_BO = 0, 128, 256, 384, 512, 640
C_DESC, C_SCALE, NCONST = 648, 664, 665


def constants():
    import math

    import numpy as np

    c = np.zeros((P, NCONST), np.float32)
    c[:, C_ID:C_ID + P] = np.eye(P)
    c[:, C_TRI:C_TRI + P] = np.triu(np.ones((P, P)), 1)
    step = 2 * math.pi / DIRS
    for j in range(DIRS):
        u = np.array([math.cos(j * step), math.sin(j * step)])
        before = np.array([math.cos((j - 1) * step), math.sin((j - 1) * step)])
        after = np.array([math.cos((j + 1) * step), math.sin((j + 1) * step)])
        p = np.array([-before[1], before[0]])
        r = np.array([-after[1], after[0]])
        p, r = p / (p @ u), r / (r @ u)
        for h in range(H):
            for d in range(DQ):
                row, col = d * H + h, h * DIRS + j
                c[KROW + row, C_KDIR + col] = u[d]
                c[row, C_PDIR + col] = p[d]
                c[row, C_RDIR + col] = r[d]
            c[h * DIRS + j, C_BO + h] = 1.0
    c[:, C_DESC:C_DESC + E] = E - np.arange(E)
    c[:, C_SCALE] = 1.0
    c[KROW:, C_SCALE] = 1.0 / math.sqrt(DQ)
    return c


def build(nc, x, consts, w_qk, b_qk, w_vr, b_v, r_b, n_w, n_w_row, w1t, b1, w2t, b2, cvec, gamma, out):
    parts_dram = nc.dram_tensor("parts_dram", [2, NROW * H, T], BF16, kind="Internal").ap()
    disp = nc.dram_tensor("disp", [SLOTS, C], F32, kind="Internal").ap()
    eout = nc.dram_tensor("eout", [SLOTS, C], F32, kind="Internal").ap()

    with ExitStack() as ctx:
        def sb(name, shape, dt=F32):
            return ctx.enter_context(nc.sbuf_tensor(name, shape, dt))

        def sem(name):
            return ctx.enter_context(nc.semaphore(name))

        y = sb("y", [P, NT, C])
        xn2 = sb("xn2", [P, NT, C])
        va = sb("va", [P, NT, H, DV + 1])
        cst = sb("cst", [P, NCONST])
        ident = cst[:, C_ID:C_ID + P]
        desc = cst[:, C_DESC:C_DESC + E]
        cbf = sb("cbf", [P, C_DESC], BF16)
        wqk = sb("wqk", [P, PROWS])
        bqk = sb("bqk", [P, 1])
        wvr = sb("wvr", [P, C + E])
        bvr = sb("bvr", [1, C + E])
        rb = sb("rb", [P, E])
        nw = sb("nw", [P, 1])
        nwr = sb("nwr", [P, C])
        gam = sb("gam", [P, 1])
        cv = sb("cv", [P, 2, C])
        b1s = sb("b1s", [P, 2, FC])
        ones1 = sb("ones1", [1, P])
        onesb = sb("onesb", [P, P], BF16)
        bst = sb("bst", [P, NT, 6])
        st = sb("st", [P, 8, NT])
        (mean, var, rstd, r2, s4, s5, s6, s7) = (st[:, k, :] for k in range(8))
        xs = sb("xs", [P, 2, GT, C])

        parts = sb("parts", [P, 2, 3, GW], BF16)
        hat1 = sb("hat1", [P, GW], BF16)
        hat = sb("hat", [P, GW], BF16)
        hatm = sb("hatm", [P, GW], BF16)
        kmax = sb("kmax", [P, 1])
        ub = sb("ub", [H, GW])
        shift = sb("shift", [H, 2, GW], BF16)
        kz = sb("kz", [P, NHG, HG, M], BF16)
        q1 = sb("q1", [P, NHG, M], BF16)
        q2 = sb("q2", [P, NHG, M], BF16)
        vp = sb("vp", [P, NHG, TB, HG, 32])
        pr = sb("pr", [P, 2, HG, M])
        ot = sb("ot", [P, M])
        rg = sb("rg", [P, TB, HG])
        att = sb("att", [P, TB, HG, DV])
        rowones = sb("rowones", [1, M], BF16)
        xnt, v32 = (pr[:, 1, k, :].rearrange("p (u m) -> p u m", u=2) for k in range(2))
        rem = ot[:].rearrange("p (u m) -> p u m", u=2)
        lg = sb("lg", [P, NT, E])
        idx = sb("idx", [P, 2, NT], I32)
        idxs = sb("idxs", [P, 2, TB], I32)
        co = sb("co", [P, 5, NT])
        pflat = parts[:].rearrange("p u k m -> p (u k m)").bitcast(F32)
        small = pflat[:, 0:12 * NT].rearrange("p (k t) -> p k t", t=NT)
        big = pr[:, 0, :, :]
        cntb = pr[:, 1, 0, :].bitcast(BF16)
        w1 = kz[:, 0, :, :].rearrange("p g m -> p (g m)").bitcast(F32)
        ef = pr[:, :, :, :].rearrange("p a b m -> p (a b) m")
        hs, dt_, dd, yo = ef[:, 0:4, :], ef[:, 4, :], ef[:, 5:7, :], ef[:, 7, :]
        b2s = pflat[:, 0:2 * C].rearrange("p (u c) -> p u c", c=C)
        g1 = xs[:].rearrange("p u t c -> p (u t) c").rearrange("p (k c2) c -> p k c2 c", c2=2)

        ps = ctx.enter_context(nc.psum_tensor("ps", [P, 8, HALF], F32))
        ps_t, ps_qk, ps_v, ps_ku, ps_p = ps[:, 0, :], ps[:, 1, :], ps[:, 2:4, :], ps[:, 4:6, :], ps[:, 6:8, :]
        ps_s = [ps[:, 0:2, :], ps[:, 2:4, :]]
        ps_acc, ps_o = ps[:, 4:6, :], ps[:, 6:8, :]

        names = ("x_in w_in zero_in const_rdy bns stat_d stat_a stat_rdy xn_rdy tr_rdy xnt_rdy proj_rdy "
                 "v_rdy y_upd hi_rdy rem_rdy mid_rdy lo_rdy xn2_a xn2_rdy v_evac lg_rdy parts_out0 parts_out1 ku_rdy kmax_rdy "
                 "p_rdy hat1_rdy hat_a hat_rdy u_rdy ub_rdy shift_rdy shift_out0 shift_out1 "
                 "half route rpool r_exp cnt_rdy pos_rdy ztile init_rdy kz_init "
                 "ld0 ld1 vp_rdy s1 relu s2 exps pv acc_evac o_rdy rg_rdy att_rdy y_att "
                 "scat staged pool_step carry "
                 "ed0 ed1 etr edt fc1 gel fc2 yo_rdy yo_out gath0 gath1 gath2 gath3 comb final").split()
        S = {n: sem(n) for n in names}

        block = ctx.enter_context(nc.Block())
        DV1 = DV + 1
        NLOAD = 16 * 3 * HG
        GS = 2 * NT
        ONE = 1
        FROM_ONE = ("xnt_rdy v_rdy v_evac lg_rdy kmax_rdy shift_rdy parts_out0 parts_out1 shift_out0 shift_out1 tr_rdy xn2_a "
                    "exps acc_evac att_rdy o_rdy y_att gel yo_rdy yo_out").split()
        PV0 = NHG * TB
        LO0 = 1
        CO0 = 4

        @block.sync
        def _(sp):
            with sp.Fori(0, B) as b:
                sp.dma_start(y[:, bass.ts(b, TB), :],
                             x[bass.ts(b, M), :].rearrange("(t p) c -> p t c", p=P)).then_inc(S["x_in"], 16)
            for dst, src in ((cst[:], consts), (wqk[:], w_qk), (bqk[0:PROWS, :], b_qk), (wvr[:], w_vr),
                             (bvr[:, 0:C], b_v), (rb[:], r_b.partition_broadcast(P)), (nw[:], n_w),
                             (nwr[:], n_w_row.partition_broadcast(P)), (gam[:], gamma.partition_broadcast(P)),
                             (cv[:], cvec.partition_broadcast(P))):
                sp.dma_start(dst, src).then_inc(S["w_in"], 16)
            sp.wait_ge(S["init_rdy"], 1)
            sp.wait_ge(S["ztile"], 2)
            for hg in range(NHG):
                for g in range(HG):
                    r = 32 * g + NPROD
                    sp.dma_start(kz[r:r + 1, hg, g, :], rowones[:]).then_inc(S["kz_init"], 16)
            for e in range(E_MLP):
                sp.dma_start(disp[e * CAP:(e + 1) * CAP, :].rearrange("(p j) c -> p (j c)", p=P),
                             pr[:, 0, 3, :]).then_inc(S["zero_in"], 16)
            with sp.Fori(0, B) as b:
                for u in range(2):
                    cols = bass.ds(b * M + u * GW, GW)
                    sp.wait_ge(S["lo_rdy"], LO0 + 2 * b + u + 1)
                    sp.dma_start(parts_dram[0, 0:NPROD * H, cols].rearrange("(i p) t -> p i t", i=3),
                                 parts[0:3 * QP, u, :, :]).then_inc(S[f"parts_out{u}"], 16)
                    for i in range(3):
                        r = i * 3 * QP
                        sp.dma_start(parts_dram[1, r:r + 3 * QP, cols].rearrange("(x p) t -> p x t", x=3),
                                     parts[KROW + i * QP:KROW + (i + 1) * QP, u, :, :]).then_inc(S[f"parts_out{u}"], 16)
                for u in range(2):
                    sp.wait_ge(S["shift_rdy"], ONE + 2 * b + u + 1)
                    sp.dma_start(parts_dram[0, NPROD * H:NROW * H, bass.ds(b * M + u * GW, GW)],
                                 shift[:, u, :]).then_inc(S[f"shift_out{u}"], 16)
            for u in range(2):
                sp.wait_ge(S[f"parts_out{u}"], ONE + 64 * B)
                sp.wait_ge(S[f"shift_out{u}"], ONE + 16 * B)
            sp.wait_ge(S["kz_init"], 16 * NHG * HG)
            with sp.Fori(0, B) as b:
                for hg in range(NHG):
                    sp.wait_ge(S["pv"], NHG * TB * b + (hg + 1) * TB)
                    for g in range(HG):
                        h = hg * HG + g
                        tok = bass.ts(b, M)
                        krows = parts_dram[1, :, tok].rearrange("(r h) t -> h r t", h=H)[h]
                        qrows = parts_dram[0, :, tok].rearrange("(r h) t -> h r t", h=H)[h]
                        r = 32 * g
                        sp.dma_start(kz[r:r + NPROD, hg, g, :], krows[0:NPROD, :]).then_inc(S[f"ld{hg}"], 16)
                        sp.dma_start(q1[r:r + NPROD, hg, :], qrows[0:NPROD, :]).then_inc(S[f"ld{hg}"], 16)
                        sp.dma_start(q2[r:r + NROW, hg, :], qrows).then_inc(S[f"ld{hg}"], 16)
            sp.wait_ge(S["y_att"], ONE + NHG * B)
            sp.wait_ge(S["scat"], 16 * GS)
            def load_expert(e, u):
                for dst, src in ((w1[:, (2 * u) * FFN:(2 * u + 1) * FFN], w1t[bass.ds(e, 1), :, :].rearrange("a p f -> p (a f)")),
                                 (w1[:, (2 * u + 1) * FFN:(2 * u + 2) * FFN], w2t[bass.ds(e, 1), :, :].rearrange("a p f -> p (a f)")),
                                 (b1s[:, u, :], b1[bass.ds(e, 1), :, :].rearrange("a p f -> p (a f)")),
                                 (b2s[:, u, :], b2[bass.ds(e, 1), :].partition_broadcast(P)),
                                 (dd[:, u, :], disp[bass.ds(e * CAP, CAP), :].rearrange("(p j) c -> p (j c)", p=P))):
                    sp.dma_start(dst, src).then_inc(S[f"ed{u}"], 16)

            def store_expert(e):
                sp.wait_ge(S["yo_rdy"], ONE + e + 1)
                sp.dma_start(eout[bass.ds(e * CAP, CAP), :].rearrange("(p j) c -> p (j c)", p=P),
                             yo).then_inc(S["yo_out"], 16)

            for u in range(2):
                load_expert(u, u)
            with sp.Fori(0, E_MLP // 2 - 1) as k:
                for u in range(2):
                    store_expert(2 * k + u)
                    load_expert(2 * k + u + 2, u)
            for u in range(2):
                store_expert(E_MLP - 2 + u)
            with sp.Fori(0, B) as b:
                sp.wait_ge(S["comb"], CO0 + TB * (b + 1))
                sp.dma_start(out[bass.ts(b, M), :].rearrange("(t p) c -> p t c", p=P),
                             y[:, bass.ts(b, TB), :]).then_inc(S["final"], 16)
            sp.wait_ge(S["final"], 16 * B)

        @block.gpsimd
        def _(pool):
            pool.memset(ones1[:], 1.0)
            pool.memset(onesb[:], 1.0)
            pool.memset(bvr[:, C:C + E], 0.0)
            pool.memset(va[:, :, :, DV:DV1], 1.0)
            pool.memset(vp[:], 0.0).then_inc(S["init_rdy"], 1)

            with pool.Fori(0, B) as b:
                for u in range(2):
                    tiles = bass.ds(b * TB + u * GT, GT)
                    n = 2 * b + u
                    pool.wait_ge(S["xn_rdy"], n + 1)
                    pool.wait_ge(S["stat_rdy"], 1)
                    pool.tensor_tensor(xn2[:, tiles, :], xs[:, u, :, :],
                                       r2[:, tiles].unsqueeze(2).broadcast_to([P, GT, C]),
                                       ALU.mult).then_inc(S["xn2_a"], 1)
                    pool.wait_ge(S["xn2_a"], ONE + n + 1)
                    pool.sem_inc(S["carry"], 1)
                    pool.tensor_tensor(xn2[:, tiles, :], xn2[:, tiles, :],
                                       nwr[:].unsqueeze(1).broadcast_to([P, GT, C]),
                                       ALU.mult).then_inc(S["xn2_rdy"], 1)
                    pool.wait_ge(S["hi_rdy"], n + 1)
                    pool.tensor_tensor(rem[0:PROWS, u, :], v32[0:PROWS, u, :], parts[0:PROWS, u, 0, :],
                                       ALU.subtract).then_inc(S["rem_rdy"], 1)
                    pool.wait_ge(S["mid_rdy"], n + 1)
                    pool.tensor_tensor(parts[0:PROWS, u, 2, :], rem[0:PROWS, u, :], parts[0:PROWS, u, 1, :],
                                       ALU.subtract).then_inc(S["lo_rdy"], 1)
            pool.wait_ge(S["route"], 1)
            with pool.Fori(0, B) as b:
                for hg in range(NHG):
                    pool.wait_ge(S["pv"], NHG * TB * b + (hg + 1) * TB)
                    pool.wait_ge(S["v_evac"], ONE + 2 * B)
                    pool.tensor_copy(vp[:, hg, :, :, 0:DV1],
                                     va[:, bass.ts(b, TB), hg * HG:(hg + 1) * HG, :]).then_inc(S["vp_rdy"], 1)
                pool.wait_ge(S["zero_in"], 16 * E_MLP)
                pool.tensor_copy(xs[:].rearrange("p u t c -> p (u t) c"), xn2[:, bass.ds(b * TB, TB), :])
                pool.tensor_copy(idxs[:], idx[:, :, bass.ds(b * TB, TB)]).then_inc(S["staged"], 1)
                pool.wait_ge(S["staged"], b + 1)
                pool.sem_inc(S["carry"], 1)
                for t in range(TB):
                    for k in range(2):
                        pool.indirect_dma_start(
                            out=disp, out_offset=bass.IndirectOffsetOnAxis(ap=idxs[:, k, t:t + 1], axis=0),
                            in_=xs[:, t // GT, t % GT, :], in_offset=None,
                            bounds_check=SLOTS - 1, oob_is_err=False).then_inc(S["scat"], 16)
                for hg in range(NHG):
                    pool.wait_ge(S["att_rdy"], ONE + NHG * b + hg + 1)
                    pool.wait_ge(S["route"], 1)
                    ys = y[:, bass.ts(b, TB), hg * HG * DV:(hg + 1) * HG * DV]
                    pool.tensor_tensor(ys, ys, att[:, :, :, :].rearrange("p t g d -> p t (g d)"),
                                       ALU.add).then_inc(S["y_att"], 1)
                pool.wait_ge(S["scat"], 16 * 2 * TB * (b + 1))
            with pool.Fori(0, B) as b:
                tiles = bass.ds(b * TB, TB)
                pool.wait_ge(S["scat"], 16 * GS)
                xb, yb = xn2[:, tiles, :], y[:, tiles, :]

                for k in range(3):
                    weight = co[:, 2 + k, tiles].unsqueeze(2).broadcast_to([P, TB, C])
                    what = xb if k == 0 else cv[:, k - 1, :].unsqueeze(1).broadcast_to([P, TB, C])
                    pool.tensor_tensor(xb, what, weight, ALU.mult).then_inc(S["pool_step"], 1)
                    pool.wait_ge(S["pool_step"], 6 * b + 2 * k + 1)
                    pool.sem_inc(S["carry"], 1)
                    pool.tensor_tensor(yb, yb, xb, ALU.add).then_inc(S["pool_step"], 1)
                    pool.wait_ge(S["pool_step"], 6 * b + 2 * k + 2)
                    pool.sem_inc(S["carry"], 1)
            pool.wait_ge(S["yo_out"], ONE + 16 * E_MLP)
            with pool.Fori(0, B) as b:
                pool.tensor_copy(idxs[:], idx[:, :, bass.ds(b * TB, TB)]).then_inc(S["staged"], 1)
                pool.wait_ge(S["staged"], B + b + 1)
                for t in range(TB):
                    k = t % 4
                    pool.wait_ge(S["comb"], TB * b + t + 1)
                    pool.sem_inc(S["carry"], 1)
                    for c in range(2):
                        pool.indirect_dma_start(
                            out=g1[:, k, c, :], out_offset=None, in_=eout,
                            in_offset=bass.IndirectOffsetOnAxis(ap=idxs[:, c, t:t + 1], axis=0),
                            bounds_check=SLOTS - 1, oob_is_err=False).then_inc(S[f"gath{k}"], 16)
                for k in range(4):
                    pool.wait_ge(S[f"gath{k}"], 64 * (b + 1))

        @block.scalar
        def _(act):
            act.wait_ge(S["stat_d"], 1)
            act.activation(rstd, s4, ACT.Sqrt).then_inc(S["stat_a"], 1)
            act.wait_ge(S["stat_d"], 2)
            act.activation(r2, s5, ACT.Sqrt).then_inc(S["stat_a"], 1)
            act.wait_ge(S["init_rdy"], 1)
            with act.Fori(0, B) as b:
                for u in range(2):
                    n = 2 * b + u
                    act.wait_ge(S["tr_rdy"], ONE + n + 1)
                    act.copy(xnt[:, u, :], ps_t).then_inc(S["xnt_rdy"], 1)
                    act.wait_ge(S["proj_rdy"], n + 1)
                    for half in range(2):
                        last = act.copy(va[:, bass.ds(b * TB + u * GT + 2 * half, 2), :, 0:DV],
                                        ps_v[:, half, :].rearrange("p (t c) -> p t c", t=2)[:, :, 0:C]
                                        .rearrange("p t (h d) -> p t h d", h=H))
                    last.then_inc(S["v_evac"], 1)
                    act.wait_ge(S["v_rdy"], ONE + n + 1)
                    act.wait_ge(S[f"parts_out{u}"], ONE + 64 * b)
                    act.copy(parts[0:PROWS, u, 0, :], v32[0:PROWS, u, :]).then_inc(S["hi_rdy"], 1)
                    act.wait_ge(S["rem_rdy"], n + 1)
                    act.copy(parts[0:PROWS, u, 1, :], rem[0:PROWS, u, :]).then_inc(S["mid_rdy"], 1)
                for u in range(2):
                    n = 2 * b + u
                    act.wait_ge(S["p_rdy"], n + 1)
                    act.copy(hat1[:], ps_p[:, 0, :]).then_inc(S["hat1_rdy"], 1)
                    act.wait_ge(S["u_rdy"], n + 1)
                    act.mul(ub[:], ps_p[0:H, 0, :], -1.0).then_inc(S["ub_rdy"], 1)
            act.wait_ge(S["rpool"], 1)
            act.activation(big[:, 1, :], big[:, 0, :], ACT.Exp).then_inc(S["r_exp"], 1)
            act.wait_ge(S["route"], 1)
            with act.Fori(0, B) as b:
                for n in range(NHG * TB * HG):
                    kc, g = n // HG, n % HG
                    act.wait_ge(S["s2"], b * NHG * TB * HG + n + 1)
                    if g == 0:
                        act.wait_ge(S["pv"], PV0 + NHG * TB * b + kc - 1)
                    act.activation(pr[:, kc % 2, g, :], ps_s[n % 2].rearrange("p a m -> p (a m)"), ACT.Exp,
                                   scale=SLOPE).then_inc(S["exps"], 1)
            with act.Fori(0, E_MLP // 2) as k:
                for u in range(2):
                    e = 2 * k + u
                    for half in range(2):
                        act.wait_ge(S["etr"], 2 * e + half + 1)
                        act.copy(dt_[:, half * HALF:(half + 1) * HALF], ps[:, half, :]).then_inc(S["edt"], 1)
                    for f in range(FC):
                        for half in range(2):
                            n = f * 2 + half
                            act.wait_ge(S["fc1"], 8 * e + n + 1)
                            act.activation(hs[:, f, half * HALF:(half + 1) * HALF], ps[:, 2 + n % 4, :], ACT.Gelu,
                                           bias=b1s[:, u, f:f + 1]).then_inc(S["gel"], 1)

        @block.tensor
        def _(pe):
            pe.sem_inc(S["pv"], PV0)
            pe.wait_ge(S["const_rdy"], 2)
            pe.wait_ge(S["init_rdy"], 1)
            with pe.Fori(0, B) as b:
                for u in range(2):
                    n = 2 * b + u
                    pe.wait_ge(S["xn_rdy"], n + 1)
                    pe.wait_ge(S["xnt_rdy"], ONE + n)
                    for t in range(GT):
                        last = pe.transpose(ps_t[:, t * P:(t + 1) * P], xs[:, u, t, :], ident)
                    last.then_inc(S["tr_rdy"], 1)
                    pe.wait_ge(S["xnt_rdy"], ONE + n + 1)
                    pe.wait_ge(S["v_rdy"], ONE + n)
                    pe.wait_ge(S["v_evac"], ONE + n)
                    pe.wait_ge(S["lg_rdy"], ONE + n)
                    pe.matmul(ps_qk[0:PROWS, :], wqk[:], xnt[:, u, :], start=True, stop=True)
                    for t in range(GT):
                        o = ps_v[:, t // 2, (t % 2) * 256:(t % 2) * 256 + C + E]
                        pe.matmul(o, xnt[:, u, t * P:(t + 1) * P], wvr[:], start=True, stop=False)
                        last = pe.matmul(o, ones1[:], bvr[:], start=False, stop=True)
                    last.then_inc(S["proj_rdy"], 1)
                    pe.wait_ge(S["hi_rdy"], n + 1)
                    pe.wait_ge(S["kmax_rdy"], ONE + b)
                    pe.matmul(ps_ku[:, u, :], cbf[KROW:KROW + QP, C_KDIR:C_KDIR + P], parts[KROW:KROW + QP, u, 0, :],
                              start=True, stop=True).then_inc(S["ku_rdy"], 1)
                for u in range(2):
                    n = 2 * b + u
                    pe.wait_ge(S["shift_rdy"], ONE + n)
                    pe.matmul(ps_p[:, 0, :], cbf[0:QP, C_PDIR:C_PDIR + P], parts[0:QP, u, 0, :], start=True, stop=True)
                    pe.matmul(ps_p[:, 1, :], cbf[0:QP, C_RDIR:C_RDIR + P], parts[0:QP, u, 0, :], start=True,
                              stop=True).then_inc(S["p_rdy"], 1)
                    pe.wait_ge(S["hat_rdy"], n + 1)
                    pe.matmul(ps_p[0:H, 0, :], cbf[:, C_BO:C_BO + H], hatm[:], start=True,
                              stop=True).then_inc(S["u_rdy"], 1)
            pe.wait_ge(S["cnt_rdy"], 1)
            for half in range(2):
                cols = slice(half * HALF, (half + 1) * HALF)
                pe.matmul(ps[:, half, :], cbf[:, C_TRI:C_TRI + P], cntb[:, 0:1024][:, cols], start=True, stop=False)
                last = pe.matmul(ps[:, half, :], onesb[:], cntb[:, 1024:2048][:, cols], start=False, stop=True)
            last.then_inc(S["pos_rdy"], 1)
            pe.wait_ge(S["route"], 1)
            NS = TB * HG
            with pe.Fori(0, B) as b:
                base = b * NHG * NS

                def scores(n):
                    hg, kc, g = n // NS, n % NS // HG, n % HG
                    if n % NS == 0:
                        pe.wait_ge(S[f"ld{hg}"], NLOAD * (b + 1))
                    if n >= 2:
                        pe.wait_ge(S["exps"], ONE + base + n - 1)
                    else:
                        pe.wait_ge(S["exps"], ONE + base)
                    for half in range(2):
                        last = pe.matmul(ps_s[n % 2][:, half, :], kz[:, hg, g, kc * P:(kc + 1) * P],
                                         q1[:, hg, half * HALF:(half + 1) * HALF], start=True, stop=True)
                    last.then_inc(S["s1"], 1)

                def shifted(n):
                    hg, kc, g = n // NS, n % NS // HG, n % HG
                    pe.wait_ge(S["relu"], base + n + 1)
                    for half in range(2):
                        last = pe.matmul(ps_s[n % 2][:, half, :], kz[:, hg, g, kc * P:(kc + 1) * P],
                                         q2[:, hg, half * HALF:(half + 1) * HALF], start=False, stop=True,
                                         skip_group_check=True)
                    last.then_inc(S["s2"], 1)

                def values(c):
                    hg, kc = c // TB, c % TB
                    pe.wait_ge(S["exps"], ONE + base + HG * (c + 1))
                    if kc == 0:
                        pe.wait_ge(S["vp_rdy"], NHG * b + hg + 1)
                        pe.wait_ge(S["acc_evac"], ONE + NHG * b + hg)
                    for half in range(2):
                        for g in range(HG):
                            last = pe.matmul(ps_acc[32 * g:32 * g + 32, half, :], vp[:, hg, kc, g, :],
                                             pr[:, c % 2, g, half * HALF:(half + 1) * HALF],
                                             start=(kc == 0), stop=(kc == TB - 1), tile_position=(0, 32 * g))
                    last.then_inc(S["pv"], 1)

                def turn(hg):
                    pe.wait_ge(S["acc_evac"], ONE + NHG * b + hg + 1)
                    pe.wait_ge(S["att_rdy"], ONE + NHG * b + hg)
                    for t in range(TB):
                        last = pe.transpose(ps_o[:, t // 4, (t % 4) * P:(t % 4 + 1) * P], ot[:, t * P:(t + 1) * P],
                                            ident)
                    last.then_inc(S["o_rdy"], 1)

                N = NHG * NS
                scores(0)
                for n in range(N):
                    if n + 1 < N:
                        scores(n + 1)
                    shifted(n)
                    if n % HG == 1 and n > HG:
                        values(n // HG - 1)
                    if n == NS + 4:
                        turn(0)
                values(NHG * TB - 1)
                turn(1)
            pe.wait_ge(S["y_att"], ONE + NHG * B)
            with pe.Fori(0, E_MLP // 2) as k:
                for u in range(2):
                    e = 2 * k + u
                    pe.wait_ge(S[f"ed{u}"], 80 * (k + 1))
                    for half in range(2):
                        for t in range(4):
                            j = half * 4 + t
                            last = pe.transpose(ps[:, half, t * P:(t + 1) * P], dd[:, u, j * P:(j + 1) * P], ident)
                        last.then_inc(S["etr"], 1)
                    pe.wait_ge(S["edt"], 2 * (e + 1))
                    pe.wait_ge(S["gel"], ONE + 8 * e)
                    for f in range(FC):
                        for half in range(2):
                            n = f * 2 + half
                            if n >= 4:
                                pe.wait_ge(S["gel"], ONE + 8 * e + n - 3)
                            pe.matmul(ps[:, 2 + n % 4, :], w1[:, 2 * u * FFN + f * P:2 * u * FFN + (f + 1) * P],
                                      dt_[:, half * HALF:(half + 1) * HALF], start=True, stop=True
                                      ).then_inc(S["fc1"], 1)
                    pe.wait_ge(S["gel"], ONE + 8 * (e + 1))
                    pe.wait_ge(S["yo_rdy"], ONE + e)
                    for j in range(ST):
                        o = ps[:, 6 + j // 4, (j % 4) * P:(j % 4 + 1) * P]
                        for f in range(FC):
                            last = pe.matmul(o, hs[:, f, j * P:(j + 1) * P],
                                             w1[:, (2 * u + 1) * FFN + f * P:(2 * u + 1) * FFN + (f + 1) * P],
                                             start=(f == 0), stop=(f == FC - 1))
                    last.then_inc(S["fc2"], 1)

        @block.vector
        def _(dve):
            step = [0]
            stat = S["bns"]

            def link(ins):
                step[0] += 1
                ins.then_inc(stat, 1)
                dve.wait_ge(stat, step[0])

            for name in FROM_ONE:
                dve.sem_inc(S[name], ONE)
            dve.sem_inc(S["lo_rdy"], LO0)
            dve.sem_inc(S["comb"], CO0)
            dve.memset(rowones[:], 1.0)
            dve.memset(kz[:].rearrange("p a b m -> p (a b m)").bitcast(F32), 0.0)
            dve.memset(q1[:].rearrange("p a m -> p (a m)").bitcast(F32), 0.0)
            dve.memset(q2[:].rearrange("p a m -> p (a m)").bitcast(F32), 0.0).then_inc(S["ztile"], 1)
            dve.memset(pr[:, 0, 3, :], 0.0).then_inc(S["ztile"], 1)
            dve.wait_ge(S["w_in"], 16 * 10)
            dve.tensor_copy(cbf[:], cst[:, 0:C_DESC]).then_inc(S["const_rdy"], 1)
            dve.tensor_scalar(wvr[:, C:C + E], wvr[:, C:C + E], nw[:, 0:1], None, ALU.mult
                              ).then_inc(S["const_rdy"], 1)
            dve.wait_ge(S["x_in"], 16 * B)
            with dve.Fori(0, B) as b:
                for t in range(TB):
                    last = dve.bn_stats(bst[:, bass.ds(b * TB + t, 1), :].rearrange("p a s -> p (a s)"),
                                        y[:, bass.ds(b * TB + t, 1), :].rearrange("p a c -> p (a c)"))
                last.then_inc(stat, 1)
            step[0] = B
            dve.wait_ge(stat, B)
            me, se, mo, so = (bst[:, :, k] for k in (1, 2, 4, 5))
            link(dve.tensor_tensor(mean, me, mo, ALU.add))
            link(dve.tensor_tensor(s6, me, mo, ALU.subtract))
            link(dve.tensor_tensor(var, se, so, ALU.add))
            link(dve.tensor_tensor(s6, s6, s6, ALU.mult))
            link(dve.tensor_scalar(mean, mean, 0.5, None, ALU.mult))
            link(dve.tensor_scalar(var, var, 1.0 / C, None, ALU.mult))
            link(dve.scalar_tensor_tensor(out=var, in0=s6, scalar=0.25, in1=var, op0=ALU.mult, op1=ALU.add))
            dve.tensor_scalar(s4, var, EPS, None, ALU.add).then_inc(S["stat_d"], 1)
            dve.wait_ge(S["stat_a"], 1)
            link(dve.reciprocal(rstd, rstd))
            link(dve.tensor_tensor(s7, var, rstd, ALU.mult))
            link(dve.tensor_tensor(s7, s7, rstd, ALU.mult))
            dve.tensor_scalar(s5, s7, EPS, None, ALU.add).then_inc(S["stat_d"], 1)
            dve.wait_ge(S["stat_a"], 2)
            dve.reciprocal(r2, r2).then_inc(S["stat_rdy"], 1)
            dve.wait_ge(S["stat_rdy"], 1)

            with dve.Fori(0, B) as b:
                for u in range(2):
                    n = 2 * b + u
                    tiles = bass.ds(b * TB + u * GT, GT)
                    dve.wait_ge(S["tr_rdy"], ONE + n)
                    dve.wait_ge(S["xn2_a"], ONE + n)
                    for t in range(GT):
                        tt = bass.ds(b * TB + u * GT + t, 1)
                        last = dve.tensor_scalar(xs[:, u, t, :], y[:, tt, :].rearrange("p a c -> p (a c)"),
                                                 mean[:, tt], rstd[:, tt], ALU.subtract, ALU.mult)
                    last.then_inc(S["xn_rdy"], 1)
                    dve.wait_ge(S["xn_rdy"], n + 1)
                    dve.tensor_tensor(y[:, tiles, :], y[:, tiles, :], xs[:, u, :, :], ALU.add).then_inc(S["y_upd"], 1)
                    dve.wait_ge(S["proj_rdy"], n + 1)
                    dve.wait_ge(S["lo_rdy"], n)
                    dve.tensor_scalar(v32[0:PROWS, u, :], ps_qk[0:PROWS, :], bqk[0:PROWS, 0:1],
                                      cst[0:PROWS, C_SCALE:C_SCALE + 1], ALU.add, ALU.mult).then_inc(S["v_rdy"], 1)
                    dve.wait_ge(S["v_evac"], ONE + n + 1)
                    dve.tensor_tensor(lg[:, tiles, :].rearrange("p (a t) e -> p a t e", a=2),
                                      ps_v.rearrange("p a (t c) -> p a t c", t=2)[:, :, :, C:C + E],
                                      r2[:, tiles].rearrange("p (a t) -> p a t", a=2).unsqueeze(3)
                                      .broadcast_to([P, 2, 2, E]), ALU.mult).then_inc(S["lg_rdy"], 1)
                dve.wait_ge(S["ku_rdy"], 2 * b + 2)
                dve.tensor_reduce(kmax[:], ps_ku, AX.XY, ALU.max).then_inc(S["kmax_rdy"], 1)
                dve.wait_ge(S["kmax_rdy"], ONE + b + 1)
                for u in range(2):
                    n = 2 * b + u
                    dve.wait_ge(S["hat1_rdy"], n + 1)
                    dve.tensor_tensor(hat[:], ps_p[:, 1, :], hat1[:], ALU.min).then_inc(S["hat_a"], 1)
                    dve.wait_ge(S["hat_a"], n + 1)
                    dve.tensor_scalar(hatm[:], hat[:], 0.0, kmax[:, 0:1], ALU.max, ALU.mult).then_inc(S["hat_rdy"], 1)
                    dve.wait_ge(S["ub_rdy"], n + 1)
                    dve.wait_ge(S[f"shift_out{u}"], ONE + 16 * b)
                    dve.scalar_tensor_tensor(out=shift[:, u, :], in0=ps_p[0:H, 0, :], scalar=-1.0 / SLOPE, in1=ub[:],
                                             op0=ALU.mult, op1=ALU.min).then_inc(S["shift_rdy"], 1)

            big3 = [big[:, k, :].rearrange("p (t e) -> p t e", e=E) for k in range(4)]
            b4 = pr[:, 1, 2, :].rearrange("p (t e) -> p t e", e=E)
            b5 = pr[:, 1, 3, :].rearrange("p (t e) -> p t e", e=E)
            sm = [small[:, k, :] for k in range(12)]

            def per_tile(v):
                return v.unsqueeze(2).broadcast_to([P, NT, E])

            descb = desc.unsqueeze(1).broadcast_to([P, NT, E])
            dve.wait_ge(S["zero_in"], 16 * E_MLP)
            for u in range(2):
                dve.wait_ge(S[f"parts_out{u}"], ONE + 64 * B)
            dve.wait_ge(S["lg_rdy"], ONE + 2 * B)
            link(dve.tensor_tensor(lg[:], lg[:], rb[:].unsqueeze(1).broadcast_to([P, NT, E]), ALU.add))
            link(dve.tensor_reduce(sm[0], lg[:], AX.X, ALU.max))
            dve.tensor_tensor(big3[0], lg[:], per_tile(sm[0]), ALU.subtract).then_inc(S["rpool"], 1)
            dve.wait_ge(S["r_exp"], 1)
            link(dve.tensor_reduce(sm[0], big3[1], AX.X, ALU.add))
            link(dve.reciprocal(sm[1], sm[0]))
            link(dve.tensor_tensor(big3[0], big3[1], per_tile(sm[1]), ALU.mult))
            for k, prob, onehot in ((0, big3[0], big3[2]), (1, big3[1], big3[3])):
                gate, rank = sm[2 + k], sm[4 + k]
                if k:
                    link(dve.scalar_tensor_tensor(out=prob, in0=big3[2], scalar=-2.0, in1=big3[0], op0=ALU.mult,
                                                  op1=ALU.add))
                link(dve.tensor_reduce(gate, prob, AX.X, ALU.max))
                link(dve.tensor_tensor(b4, prob, per_tile(gate), ALU.is_equal))
                link(dve.tensor_tensor(b4, b4, descb, ALU.mult))
                link(dve.tensor_reduce(rank, b4, AX.X, ALU.max))
                link(dve.tensor_tensor(onehot, b4, per_tile(rank), ALU.is_equal))
            cnt = pr[:, 1, 2, :].rearrange("p (e t) -> p e t", t=NT)
            incl = pr[:, 1, 3, :]
            reset = big[:, 0, :]
            link(dve.tensor_tensor(cnt.rearrange("p e t -> p t e"), big3[2], big3[3], ALU.add))
            link(dve.memset(reset, 1.0))
            link(dve.memset(reset.rearrange("p (e t) -> p e t", t=NT)[:, :, 0:1], 0.0))
            link(dve.tensor_tensor_scan(incl, reset, pr[:, 1, 2, :], 0.0, ALU.mult, ALU.add))
            link(dve.tensor_copy(cntb[:, 0:1024], pr[:, 1, 2, :]))
            dve.tensor_tensor(cntb[:, 1024:2048], incl, pr[:, 1, 2, :], ALU.subtract).then_inc(S["cnt_rdy"], 1)
            dve.wait_ge(S["pos_rdy"], 1)
            pos = ps[:, 0:2, :].rearrange("p a m -> p (a m)").rearrange("p (e t) -> p t e", t=NT)
            for k in range(2):
                onehot, gate, rank, at, keep = big3[2 + k], sm[2 + k], sm[4 + k], sm[6 + k], sm[8 + k]
                link(dve.tensor_tensor(b5, pos, onehot, ALU.mult))
                link(dve.tensor_reduce(at, b5, AX.X, ALU.add))
                link(dve.tensor_scalar(keep, at, float(CAP), None, ALU.is_lt))
                link(dve.tensor_tensor(gate, gate, keep, ALU.mult))
            link(dve.tensor_tensor(sm[0], sm[2], sm[3], ALU.add))
            link(dve.tensor_scalar(sm[1], sm[0], 0.0, None, ALU.is_le))
            link(dve.tensor_tensor(sm[0], sm[0], sm[1], ALU.add))
            link(dve.reciprocal(sm[0], sm[0]))
            for k in range(2):
                gate, rank, at, keep = sm[2 + k], sm[4 + k], sm[6 + k], sm[8 + k]
                link(dve.tensor_tensor(gate, gate, sm[0], ALU.mult))
                link(dve.scalar_tensor_tensor(out=keep, in0=rank, scalar=float(E_MLP), in1=keep, op0=ALU.is_le,
                                              op1=ALU.mult))
                link(dve.tensor_tensor(co[:, k, :], gate, keep, ALU.mult))
                link(dve.scalar_tensor_tensor(out=at, in0=rank, scalar=-float(CAP), in1=at, op0=ALU.mult, op1=ALU.add))
                link(dve.tensor_scalar(sm[10], keep, -SKIP, SKIP + SLOTS, ALU.mult, ALU.add))
                link(dve.tensor_tensor(at, at, sm[10], ALU.add))
                link(dve.tensor_copy(idx[:, k, :], at))
            for n in range(3):
                r = float(E - 1 - n)
                link(dve.scalar_tensor_tensor(out=sm[10], in0=sm[4], scalar=r, in1=sm[2], op0=ALU.is_equal,
                                              op1=ALU.mult))
                link(dve.scalar_tensor_tensor(out=sm[11], in0=sm[5], scalar=r, in1=sm[3], op0=ALU.is_equal,
                                              op1=ALU.mult))
                last = dve.tensor_tensor(co[:, 2 + n, :], sm[10], sm[11], ALU.add)
                if n < 2:
                    link(last)
            last.then_inc(S["route"], 1)
            dve.wait_ge(S["route"], 1)

            NS = TB * HG

            def finish(b, hg):
                m = NHG * b + hg
                dve.wait_ge(S["o_rdy"], ONE + m + 1)
                dve.wait_ge(S["y_att"], ONE + m)
                o3 = ps_o.rearrange("p a (t g c) -> p (a t) g c", g=HG, c=32)
                dve.reciprocal(rg[:], o3[:, :, :, DV]).then_inc(S["rg_rdy"], 1)
                dve.wait_ge(S["rg_rdy"], 2 * m + 1)
                dve.tensor_scalar(rg[:], rg[:], gam[:, 0:1], None, ALU.mult).then_inc(S["rg_rdy"], 1)
                dve.wait_ge(S["rg_rdy"], 2 * m + 2)
                for t in range(TB):
                    last = dve.tensor_tensor(att[:, t, :, :], o3[:, t, :, 0:DV],
                                             rg[:, t, :].unsqueeze(2).broadcast_to([P, HG, DV]), ALU.mult)
                last.then_inc(S["att_rdy"], 1)

            with dve.Fori(0, B) as b:
                base = b * NHG * NS

                def evacuate(hg):
                    dve.wait_ge(S["pv"], PV0 + NHG * TB * b + (hg + 1) * TB)
                    dve.wait_ge(S["o_rdy"], ONE + NHG * b + hg)
                    dve.tensor_copy(ot[:], ps_acc.rearrange("p a m -> p (a m)")).then_inc(S["acc_evac"], 1)

                for n in range(NHG * NS):
                    dve.wait_ge(S["s1"], base + n + 1)
                    s = ps_s[n % 2].rearrange("p a m -> p (a m)")
                    dve.tensor_scalar(s, s, 0.0, 1.0 / SLOPE - 1.0, ALU.max, ALU.mult).then_inc(S["relu"], 1)
                    if n == NS + 3:
                        evacuate(0)
                    if n == NS + 7:
                        finish(b, 0)
                evacuate(1)
                finish(b, 1)

            with dve.Fori(0, E_MLP // 2) as k:
                for u in range(2):
                    e = 2 * k + u
                    dve.wait_ge(S["fc2"], e + 1)
                    dve.wait_ge(S["yo_out"], ONE + 16 * e)
                    dve.tensor_tensor(yo.rearrange("p (j c) -> p j c", c=C),
                                      ps[:, 6:8, :].rearrange("p a (j c) -> p (a j) c", c=C),
                                      b2s[:, u, :].unsqueeze(1).broadcast_to([P, ST, C]), ALU.add
                                      ).then_inc(S["yo_rdy"], 1)
            dve.wait_ge(S["pool_step"], 6 * B)
            with dve.Fori(0, NT // 4) as q:
                for k in range(4):
                    tt = bass.ds(4 * q + k, 1)
                    yt = y[:, tt, :].rearrange("p a c -> p (a c)")
                    dve.wait_ge(S[f"gath{k}"], 32 * (q + 1))
                    dve.scalar_tensor_tensor(out=yt, in0=g1[:, k, 0, :], scalar=co[:, 0, tt], in1=yt, op0=ALU.mult,
                                             op1=ALU.add).then_inc(S["half"], 1)
                    dve.wait_ge(S["half"], 4 * q + k + 1)
                    dve.scalar_tensor_tensor(out=yt, in0=g1[:, k, 1, :], scalar=co[:, 1, tt], in1=yt, op0=ALU.mult,
                                             op1=ALU.add).then_inc(S["comb"], 1)


_INS = ("x", "consts", "w_qk", "b_qk", "w_vr", "b_v", "r_b", "n_w", "n_w_row", "w1t", "b1", "w2t", "b2", "cvec",
        "gamma")


def layouts(i):
    import numpy as np

    a = {k.split("_", 1)[1]: np.asarray(v) for k, v in i.items()}
    q, k = ({n: a[f"attn_{n}{w}"].reshape(H, DQ, -1).transpose(1, 0, 2).reshape(QP, -1) for n in "Wb"} for w in "qk")
    rows = {}
    for n, width in (("W", C), ("b", 1)):
        r = np.zeros((PROWS, width), np.float32)
        r[0:3 * QP] = np.tile(q[n], (3, 1))
        r[KROW:] = np.tile(k[n], (3, 1))
        rows[n] = r
    return {
        "x": a["attn_x"].reshape(T, C),
        "consts": constants(),
        "w_qk": rows["W"].T,
        "b_qk": rows["b"],
        "w_vr": np.concatenate([a["attn_Wv"].T, a["ffn_router_weight"].T], axis=1),
        "b_v": a["attn_bv"].reshape(1, C),
        "r_b": a["ffn_router_bias"].reshape(1, E),
        "n_w": a["ffn_norm_weight"].reshape(C, 1),
        "n_w_row": a["ffn_norm_weight"].reshape(1, C),
        "w1t": a["ffn_fc1_weight"].transpose(0, 2, 1),
        "b1": a["ffn_fc1_bias"].reshape(E_MLP, FC, P).transpose(0, 2, 1),
        "w2t": a["ffn_fc2_weight"].transpose(0, 2, 1).reshape(E_MLP, FC, P, C).transpose(0, 2, 1, 3).reshape(E_MLP, P, FC * C),
        "b2": a["ffn_fc2_bias"],
        "cvec": a["ffn_constant_vectors"].reshape(1, 2, C),
        "gamma": a["attn_gamma"].reshape(1, 1),
    }


def kernel(**inputs):
    import numpy as np
    import concourse.bacc as bacc
    from concourse.bass_utils import run_bass_kernel_spmd

    nc = bacc.Bacc("TRN2", target_bir_lowering=False, num_devices=1)
    arrays, args = {}, []
    laid = layouts(inputs)
    for name in _INS:
        v = np.ascontiguousarray(laid[name])
        arrays[f"in_{name}"] = v
        args.append(nc.dram_tensor(f"in_{name}", v.shape, mybir.dt.from_np(v.dtype), kind="ExternalInput").ap())
    out = nc.dram_tensor("out", [T, C], F32, kind="ExternalOutput").ap()
    build(nc, *args, out)
    r = run_bass_kernel_spmd(nc, [arrays], core_ids=[0])
    return r.results[0]["out"].reshape(B, M, C)
```

```python
from contextlib import ExitStack

import concourse.bass as bass
from concourse import mybir

F32 = mybir.dt.float32
BF16 = mybir.dt.bfloat16
I32 = mybir.dt.int32
ALU = mybir.AluOpType
ACT = mybir.ActivationFunctionType
AX = mybir.AxisListType

P = 128
B, M, C = 8, 1024, 128
T = B * M
NT = T // P
TB = M // P
H, DV, DQ = 8, 16, 2
HG = 4
NHG = H // HG
GT = 4
GW = GT * P
HALF = 512
QP = H * DQ
KROW = 64
PROWS = KROW + 3 * QP
NPROD = 3 * 3 * DQ
NROW = NPROD + 1
DIRS = 16
E, E_MLP, FFN = 16, 12, 512
FC = FFN // P
MLP0 = E - E_MLP
CAP = T * 2 // E
SLOTS = E_MLP * CAP
ST = CAP // P
SKIP = float(1 << 20)
EPS = 1e-5
SLOPE = 0.2

BH = B // 2
NS = TB * HG
NU = NHG * NS
NJ = NU + NHG
RING = 3
COMB0, COMBS = 13, 3
VLAG = 5
TURN = 8
QW = M // 4

C_ID, C_TRI, C_KDIR, C_PDIR, C_RDIR, C_BO = 0, 128, 256, 384, 512, 640
C_DESC, C_SCALE, NCONST = 648, 664, 665


def constants():
    import math

    import numpy as np

    c = np.zeros((P, NCONST), np.float32)
    c[:, C_ID:C_ID + P] = np.eye(P)
    c[:, C_TRI:C_TRI + P] = np.triu(np.ones((P, P)), 1)
    step = 2 * math.pi / DIRS
    for j in range(DIRS):
        u = np.array([math.cos(j * step), math.sin(j * step)])
        before = np.array([math.cos((j - 1) * step), math.sin((j - 1) * step)])
        after = np.array([math.cos((j + 1) * step), math.sin((j + 1) * step)])
        p = np.array([-before[1], before[0]])
        r = np.array([-after[1], after[0]])
        p, r = p / (p @ u), r / (r @ u)
        for h in range(H):
            for d in range(DQ):
                row, col = d * H + h, h * DIRS + j
                c[KROW + row, C_KDIR + col] = u[d]
                c[row, C_PDIR + col] = p[d]
                c[row, C_RDIR + col] = r[d]
            c[h * DIRS + j, C_BO + h] = 1.0
    c[:, C_DESC:C_DESC + E] = E - np.arange(E)
    c[:, C_SCALE] = 1.0
    c[KROW:, C_SCALE] = 1.0 / math.sqrt(DQ)
    return c


def build(nc, x, consts, w_qk, b_qk, w_vr, b_v, r_b, n_w, n_w_row, w1t, b1, w2t, b2, cvec, gamma, out):
    parts_dram = nc.dram_tensor("parts_dram", [2, NROW * H, T], BF16, kind="Internal").ap()
    disp = nc.dram_tensor("disp", [SLOTS, C], F32, kind="Internal").ap()
    eout = nc.dram_tensor("eout", [SLOTS, C], F32, kind="Internal").ap()

    with ExitStack() as ctx:
        def sb(name, shape, dt=F32):
            return ctx.enter_context(nc.sbuf_tensor(name, shape, dt))

        def sem(name):
            return ctx.enter_context(nc.semaphore(name))

        y = sb("y", [P, NT, C])
        xn2 = sb("xn2", [P, NT, C])
        va = sb("va", [P, NT, H, DV + 1])
        cst = sb("cst", [P, NCONST])
        ident = cst[:, C_ID:C_ID + P]
        desc = cst[:, C_DESC:C_DESC + E]
        cbf = sb("cbf", [P, C_DESC], BF16)
        wqk = sb("wqk", [P, PROWS])
        bqk = sb("bqk", [P, 1])
        wvr = sb("wvr", [P, C + E])
        bvr = sb("bvr", [1, C + E])
        rb = sb("rb", [P, E])
        nw = sb("nw", [P, 1])
        nwr = sb("nwr", [P, C])
        gam = sb("gam", [P, 1])
        cv = sb("cv", [P, 2, C])
        b1s = sb("b1s", [P, 2, FC])
        ones1 = sb("ones1", [1, P])
        onesb = sb("onesb", [P, P], BF16)
        bst = sb("bst", [P, NT, 6])
        st = sb("st", [P, 8, NT])
        (mean, var, rstd, r2, s4, s5, s6, s7) = (st[:, k, :] for k in range(8))
        xs = sb("xs", [P, 2, GT, C])

        parts = sb("parts", [P, 2, 3, GW], BF16)
        hat1 = sb("hat1", [P, GW], BF16)
        hat = sb("hat", [P, GW], BF16)
        hatm = sb("hatm", [P, GW], BF16)
        kmax = sb("kmax", [P, 1])
        ub = sb("ub", [H, GW])
        shift = sb("shift", [H, 2, GW], BF16)
        kz = sb("kz", [P, NHG, HG, M], BF16)
        q1 = sb("q1", [P, NHG, M], BF16)
        q2 = sb("q2", [P, NHG, M], BF16)
        vp = sb("vp", [P, NHG, TB, HG, 32])
        pr = sb("pr", [P, 2, HG, M])
        ot = sb("ot", [P, M])
        rg = sb("rg", [P, TB, HG])
        att = sb("att", [P, TB, HG, DV])
        rowones = sb("rowones", [1, M], BF16)
        xnt, v32 = (pr[:, 1, k, :].rearrange("p (u m) -> p u m", u=2) for k in range(2))
        rem = ot[:].rearrange("p (u m) -> p u m", u=2)
        lg = sb("lg", [P, NT, E])
        idx = sb("idx", [P, 2, NT], I32)
        idxs = sb("idxs", [P, 2, TB], I32)
        co = sb("co", [P, 5, NT])
        pflat = parts[:].rearrange("p u k m -> p (u k m)").bitcast(F32)
        small = pflat[:, 0:12 * NT].rearrange("p (k t) -> p k t", t=NT)
        big = pr[:, 0, :, :]
        cntb = pr[:, 1, 0, :].bitcast(BF16)
        w1 = kz[:, 1, :, :].rearrange("p g m -> p (g m)").bitcast(F32)
        ef = pr[:, :, :, :].rearrange("p a b m -> p (a b) m")
        hs, dt_, dd, yo = ef[:, 0:4, :], ef[:, 4, :], ef[:, 5:7, :], ef[:, 7, :]
        b2s = pflat[:, 0:2 * C].rearrange("p (u c) -> p u c", c=C)
        g1 = xs[:].rearrange("p u t c -> p (u t) c").rearrange("p (k c2) c -> p k c2 c", c2=2)

        ps = ctx.enter_context(nc.psum_tensor("ps", [P, 8, HALF], F32))
        ps_t, ps_qk, ps_v, ps_ku, ps_p = ps[:, 0, :], ps[:, 1, :], ps[:, 2:4, :], ps[:, 4:6, :], ps[:, 6:8, :]
        ring = [ps[:, 2 * k:2 * k + 2, :] for k in range(RING)]
        ps_acc = ps[:, 6:8, :]

        names = ("x_in w_in zero_in const_rdy bns stat_d stat_a stat_rdy xn_rdy tr_rdy xnt_rdy proj_rdy "
                 "v_rdy y_upd hi_rdy rem_rdy mid_rdy lo_rdy xn2_a xn2_rdy v_evac lg_rdy parts_out0 parts_out1 ku_rdy kmax_rdy "
                 "p_rdy hat1_rdy hat_a hat_rdy u_rdy ub_rdy shift_rdy shift_out0 shift_out1 "
                 "first_row route rpool r_exp cnt_rdy pos_rdy ztile init_rdy kz_init "
                 "ld0 ld1 vp_rdy s1 relu s2 exps pv acc_evac o_rdy rg_rdy att_rdy y_att "
                 "scat staged pool_step carry "
                 "ed0 ed1 etr edt fc1 gel fc2 yo_rdy yo_out gath0 gath1 gath2 gath3 comb final").split()
        S = {n: sem(n) for n in names}

        block = ctx.enter_context(nc.Block())
        DV1 = DV + 1
        NLOAD = 16 * 3 * HG
        GS = 2 * NT

        def unit_job(n):
            return n + (n >= TURN) + (n >= NS + TURN)

        UNIT_AT = {unit_job(n): n for n in range(NU)}
        ONE = 1
        FROM_ONE = ("xnt_rdy v_rdy v_evac lg_rdy kmax_rdy shift_rdy parts_out0 parts_out1 shift_out0 shift_out1 tr_rdy xn2_a "
                    "gel yo_rdy yo_out").split()
        PV0 = NU
        LO0 = 1
        CO0 = 4


        @block.sync
        def _(sp):
            with sp.Fori(0, B) as b:
                sp.dma_start(y[:, bass.ts(b, TB), :],
                             x[bass.ts(b, M), :].rearrange("(t p) c -> p t c", p=P)).then_inc(S["x_in"], 16)
            for dst, src in ((cst[:], consts), (wqk[:], w_qk), (bqk[0:PROWS, :], b_qk), (wvr[:], w_vr),
                             (bvr[:, 0:C], b_v), (rb[:], r_b.partition_broadcast(P)), (nw[:], n_w),
                             (nwr[:], n_w_row.partition_broadcast(P)), (gam[:], gamma.partition_broadcast(P)),
                             (cv[:], cvec.partition_broadcast(P))):
                sp.dma_start(dst, src).then_inc(S["w_in"], 16)
            sp.wait_ge(S["init_rdy"], 1)
            sp.wait_ge(S["ztile"], 2)
            for hg in range(NHG):
                for g in range(HG):
                    r = 32 * g + NPROD
                    sp.dma_start(kz[r:r + 1, hg, g, :], rowones[:]).then_inc(S["kz_init"], 16)
            for e in range(E_MLP):
                sp.dma_start(disp[e * CAP:(e + 1) * CAP, :].rearrange("(p j) c -> p (j c)", p=P),
                             pr[:, 0, 3, :]).then_inc(S["zero_in"], 16)
            with sp.Fori(0, B) as b:
                for u in range(2):
                    cols = bass.ds(b * M + u * GW, GW)
                    sp.wait_ge(S["lo_rdy"], LO0 + 2 * b + u + 1)
                    sp.dma_start(parts_dram[0, 0:NPROD * H, cols].rearrange("(i p) t -> p i t", i=3),
                                 parts[0:3 * QP, u, :, :]).then_inc(S[f"parts_out{u}"], 16)
                    for i in range(3):
                        r = i * 3 * QP
                        sp.dma_start(parts_dram[1, r:r + 3 * QP, cols].rearrange("(x p) t -> p x t", x=3),
                                     parts[KROW + i * QP:KROW + (i + 1) * QP, u, :, :]).then_inc(S[f"parts_out{u}"], 16)
                for u in range(2):
                    sp.wait_ge(S["shift_rdy"], ONE + 2 * b + u + 1)
                    sp.dma_start(parts_dram[0, NPROD * H:NROW * H, bass.ds(b * M + u * GW, GW)],
                                 shift[:, u, :]).then_inc(S[f"shift_out{u}"], 16)
            for u in range(2):
                sp.wait_ge(S[f"parts_out{u}"], ONE + 64 * B)
                sp.wait_ge(S[f"shift_out{u}"], ONE + 16 * B)
            sp.wait_ge(S["kz_init"], 16 * NHG * HG)

            def load_operands(b, hg):
                sp.wait_ge(S["pv"], NU * b + (hg + 1) * NS)
                for g in range(HG):
                    h = hg * HG + g
                    tok = bass.ts(b, M)
                    krows = parts_dram[1, :, tok].rearrange("(r h) t -> h r t", h=H)[h]
                    qrows = parts_dram[0, :, tok].rearrange("(r h) t -> h r t", h=H)[h]
                    r = 32 * g
                    sp.dma_start(kz[r:r + NPROD, hg, g, :], krows[0:NPROD, :]).then_inc(S[f"ld{hg}"], 16)
                    sp.dma_start(q1[r:r + NPROD, hg, :], qrows[0:NPROD, :]).then_inc(S[f"ld{hg}"], 16)
                    sp.dma_start(q2[r:r + NROW, hg, :], qrows).then_inc(S[f"ld{hg}"], 16)

            def store_sequence(s):
                sp.wait_ge(S["comb"], CO0 + TB * (s + 1))
                sp.sem_inc(S["carry"], 1)
                sp.wait_ge(S["y_att"], NHG * (s + 1))
                sp.dma_start(out[bass.ts(s, M), :].rearrange("(t p) c -> p t c", p=P),
                             y[:, bass.ts(s, TB), :]).then_inc(S["final"], 16)

            with sp.Fori(0, BH) as b:
                for hg in range(NHG):
                    load_operands(b, hg)
            load_operands(BH, 0)
            sp.wait_ge(S["pv"], PV0 + NU * BH)
            sp.wait_ge(S["scat"], 16 * GS)

            def load_expert(e, u):
                for dst, src in ((w1[:, (2 * u) * FFN:(2 * u + 1) * FFN], w1t[bass.ds(e, 1), :, :].rearrange("a p f -> p (a f)")),
                                 (w1[:, (2 * u + 1) * FFN:(2 * u + 2) * FFN], w2t[bass.ds(e, 1), :, :].rearrange("a p f -> p (a f)")),
                                 (b1s[:, u, :], b1[bass.ds(e, 1), :, :].rearrange("a p f -> p (a f)")),
                                 (b2s[:, u, :], b2[bass.ds(e, 1), :].partition_broadcast(P)),
                                 (dd[:, u, :], disp[bass.ds(e * CAP, CAP), :].rearrange("(p j) c -> p (j c)", p=P))):
                    sp.dma_start(dst, src).then_inc(S[f"ed{u}"], 16)

            def store_expert(e):
                sp.wait_ge(S["yo_rdy"], ONE + e + 1)
                sp.dma_start(eout[bass.ds(e * CAP, CAP), :].rearrange("(p j) c -> p (j c)", p=P),
                             yo).then_inc(S["yo_out"], 16)

            for u in range(2):
                load_expert(u, u)
            with sp.Fori(0, E_MLP // 2 - 1) as k:
                for u in range(2):
                    store_expert(2 * k + u)
                    load_expert(2 * k + u + 2, u)
            for u in range(2):
                store_expert(E_MLP - 2 + u)
            sp.wait_ge(S["ztile"], 3)
            for g in range(HG):
                r = 32 * g + NPROD
                sp.dma_start(kz[r:r + 1, 1, g, :], rowones[:]).then_inc(S["kz_init"], 16)
            sp.wait_ge(S["kz_init"], 16 * (NHG + 1) * HG)
            load_operands(BH, 1)
            with sp.Fori(1, BH) as k:
                for hg in range(NHG):
                    load_operands(k + BH, hg)
                for u in range(2):
                    store_sequence(2 * k - 2 + u)
            for u in range(2):
                store_sequence(B - 2 + u)
            sp.wait_ge(S["final"], 16 * B)

        @block.gpsimd
        def _(pool):
            pool.memset(ones1[:], 1.0)
            pool.memset(onesb[:], 1.0)
            pool.memset(bvr[:, C:C + E], 0.0)
            pool.memset(va[:, :, :, DV:DV1], 1.0)
            pool.memset(vp[:], 0.0).then_inc(S["init_rdy"], 1)

            with pool.Fori(0, B) as b:
                for u in range(2):
                    tiles = bass.ds(b * TB + u * GT, GT)
                    n = 2 * b + u
                    pool.wait_ge(S["xn_rdy"], n + 1)
                    pool.wait_ge(S["stat_rdy"], 1)
                    pool.tensor_tensor(xn2[:, tiles, :], xs[:, u, :, :],
                                       r2[:, tiles].unsqueeze(2).broadcast_to([P, GT, C]),
                                       ALU.mult).then_inc(S["xn2_a"], 1)
                    pool.wait_ge(S["xn2_a"], ONE + n + 1)
                    pool.sem_inc(S["carry"], 1)
                    pool.tensor_tensor(xn2[:, tiles, :], xn2[:, tiles, :],
                                       nwr[:].unsqueeze(1).broadcast_to([P, GT, C]),
                                       ALU.mult).then_inc(S["xn2_rdy"], 1)
                    pool.wait_ge(S["hi_rdy"], n + 1)
                    pool.tensor_tensor(rem[0:PROWS, u, :], v32[0:PROWS, u, :], parts[0:PROWS, u, 0, :],
                                       ALU.subtract).then_inc(S["rem_rdy"], 1)
                    pool.wait_ge(S["mid_rdy"], n + 1)
                    pool.tensor_tensor(parts[0:PROWS, u, 2, :], rem[0:PROWS, u, :], parts[0:PROWS, u, 1, :],
                                       ALU.subtract).then_inc(S["lo_rdy"], 1)
            pool.wait_ge(S["route"], 1)
            pool.wait_ge(S["v_evac"], ONE + 2 * B)
            pool.wait_ge(S["zero_in"], 16 * E_MLP)

            def value_rows(b, hg):
                pool.wait_ge(S["pv"], NU * b + (hg + 1) * NS)
                pool.tensor_copy(vp[:, hg, :, :, 0:DV1],
                                 va[:, bass.ts(b, TB), hg * HG:(hg + 1) * HG, :]).then_inc(S["vp_rdy"], 1)

            def add_attention(b, hg):
                pool.wait_ge(S["att_rdy"], NHG * b + hg + 1)
                pool.sem_inc(S["carry"], 1)
                ys = y[:, bass.ts(b, TB), hg * HG * DV:(hg + 1) * HG * DV]
                pool.tensor_tensor(ys, ys, att[:, :, :, :].rearrange("p t g d -> p t (g d)"),
                                   ALU.add).then_inc(S["y_att"], 1)

            def stage(s, count):
                pool.tensor_copy(idxs[:], idx[:, :, bass.ds(s * TB, TB)]).then_inc(S["staged"], 1)
                pool.wait_ge(S["staged"], count)
                pool.sem_inc(S["carry"], 1)

            def scatter(s):
                pool.tensor_copy(xs[:].rearrange("p u t c -> p (u t) c"), xn2[:, bass.ds(s * TB, TB), :])
                stage(s, s + 1)
                for t in range(TB):
                    for k in range(2):
                        pool.indirect_dma_start(
                            out=disp, out_offset=bass.IndirectOffsetOnAxis(ap=idxs[:, k, t:t + 1], axis=0),
                            in_=xs[:, t // GT, t % GT, :], in_offset=None,
                            bounds_check=SLOTS - 1, oob_is_err=False).then_inc(S["scat"], 16)
                pool.wait_ge(S["scat"], 16 * 2 * TB * (s + 1))

            def gather(s):
                stage(s, B + s + 1)
                for t in range(TB):
                    k = t % 4
                    pool.wait_ge(S["comb"], TB * s + t + 1)
                    pool.sem_inc(S["carry"], 1)
                    for c in range(2):
                        pool.indirect_dma_start(
                            out=g1[:, k, c, :], out_offset=None, in_=eout,
                            in_offset=bass.IndirectOffsetOnAxis(ap=idxs[:, c, t:t + 1], axis=0),
                            bounds_check=SLOTS - 1, oob_is_err=False).then_inc(S[f"gath{k}"], 16)
                for k in range(4):
                    pool.wait_ge(S[f"gath{k}"], 64 * (s + 1))

            def sequence(b, move, k, last):
                value_rows(b, 1)
                for u in range(2):
                    move(2 * k + u)
                if not last:
                    value_rows(b + 1, 0)
                if move is gather:
                    pool.wait_ge(S["comb"], CO0 + 2 * TB * (k + 1))
                add_attention(b, 0)
                add_attention(b, 1)

            value_rows(0, 0)
            with pool.Fori(0, BH - 1) as b:
                sequence(b, scatter, b, False)
            sequence(BH - 1, scatter, BH - 1, True)
            value_rows(BH, 0)
            with pool.Fori(0, B) as b:
                tiles = bass.ds(b * TB, TB)
                pool.wait_ge(S["scat"], 16 * GS)
                xb, yb = xn2[:, tiles, :], y[:, tiles, :]

                for k in range(3):
                    weight = co[:, 2 + k, tiles].unsqueeze(2).broadcast_to([P, TB, C])
                    what = xb if k == 0 else cv[:, k - 1, :].unsqueeze(1).broadcast_to([P, TB, C])
                    pool.tensor_tensor(xb, what, weight, ALU.mult).then_inc(S["pool_step"], 1)
                    pool.wait_ge(S["pool_step"], 6 * b + 2 * k + 1)
                    pool.sem_inc(S["carry"], 1)
                    pool.tensor_tensor(yb, yb, xb, ALU.add).then_inc(S["pool_step"], 1)
                    pool.wait_ge(S["pool_step"], 6 * b + 2 * k + 2)
                    pool.sem_inc(S["carry"], 1)
            pool.wait_ge(S["yo_out"], ONE + 16 * E_MLP)
            with pool.Fori(0, BH - 1) as k:
                sequence(k + BH, gather, k, False)
            sequence(B - 1, gather, BH - 1, True)

        @block.scalar
        def _(act):
            act.wait_ge(S["stat_d"], 1)
            act.activation(rstd, s4, ACT.Sqrt).then_inc(S["stat_a"], 1)
            act.wait_ge(S["stat_d"], 2)
            act.activation(r2, s5, ACT.Sqrt).then_inc(S["stat_a"], 1)
            act.wait_ge(S["init_rdy"], 1)
            with act.Fori(0, B) as b:
                for u in range(2):
                    n = 2 * b + u
                    act.wait_ge(S["tr_rdy"], ONE + n + 1)
                    act.copy(xnt[:, u, :], ps_t).then_inc(S["xnt_rdy"], 1)
                    act.wait_ge(S["proj_rdy"], n + 1)
                    for half in range(2):
                        last = act.copy(va[:, bass.ds(b * TB + u * GT + 2 * half, 2), :, 0:DV],
                                        ps_v[:, half, :].rearrange("p (t c) -> p t c", t=2)[:, :, 0:C]
                                        .rearrange("p t (h d) -> p t h d", h=H))
                    last.then_inc(S["v_evac"], 1)
                    act.wait_ge(S["v_rdy"], ONE + n + 1)
                    act.wait_ge(S[f"parts_out{u}"], ONE + 64 * b)
                    act.copy(parts[0:PROWS, u, 0, :], v32[0:PROWS, u, :]).then_inc(S["hi_rdy"], 1)
                    act.wait_ge(S["rem_rdy"], n + 1)
                    act.copy(parts[0:PROWS, u, 1, :], rem[0:PROWS, u, :]).then_inc(S["mid_rdy"], 1)
                for u in range(2):
                    n = 2 * b + u
                    act.wait_ge(S["p_rdy"], n + 1)
                    act.copy(hat1[:], ps_p[:, 0, :]).then_inc(S["hat1_rdy"], 1)
                    act.wait_ge(S["u_rdy"], n + 1)
                    act.mul(ub[:], ps_p[0:H, 0, :], -1.0).then_inc(S["ub_rdy"], 1)
            act.wait_ge(S["rpool"], 1)
            act.activation(big[:, 1, :], big[:, 0, :], ACT.Exp).then_inc(S["r_exp"], 1)
            act.wait_ge(S["route"], 1)

            def evacuate(b, hg, half):
                act.wait_ge(S["pv"], PV0 + NU * b + NS * hg + NS - 4 + 2 * (half + 1))
                if not (isinstance(b, int) and NHG * b + hg < 1):
                    act.wait_ge(S["o_rdy"], NHG * b + hg)
                act.copy(ot[:, half * HALF:(half + 1) * HALF], ps_acc[:, half, :]).then_inc(S["acc_evac"], 1)

            def sequence(b, first):
                for n in range(NU):
                    kc, g = n // HG, n % HG
                    if n % NS in (2, 4) and not (first and n < NS):
                        evacuate(b - (n < NS), (n // NS + 1) % NHG, n % NS // 2 - 1)
                    act.wait_ge(S["s2"], NU * b + n + 1)
                    if g == 0:
                        act.wait_ge(S["pv"], PV0 + NU * b + HG * (kc - 1))
                    act.activation(pr[:, kc % 2, g, :], ring[unit_job(n) % RING].rearrange("p a m -> p (a m)"),
                                   ACT.Exp, scale=SLOPE).then_inc(S["exps"], 1)

            def attention(b0):
                sequence(b0, True)
                with act.Fori(b0 + 1, b0 + BH) as b:
                    sequence(b, False)
                for half in range(2):
                    evacuate(b0 + BH - 1, NHG - 1, half)

            attention(0)
            with act.Fori(0, E_MLP // 2) as k:
                for u in range(2):
                    e = 2 * k + u
                    for half in range(2):
                        act.wait_ge(S["etr"], 2 * e + half + 1)
                        act.copy(dt_[:, half * HALF:(half + 1) * HALF], ps[:, half, :]).then_inc(S["edt"], 1)
                    for f in range(FC):
                        for half in range(2):
                            n = f * 2 + half
                            act.wait_ge(S["fc1"], 8 * e + n + 1)
                            act.activation(hs[:, f, half * HALF:(half + 1) * HALF], ps[:, 2 + n % 4, :], ACT.Gelu,
                                           bias=b1s[:, u, f:f + 1]).then_inc(S["gel"], 1)
            act.wait_ge(S["yo_out"], ONE + 16 * E_MLP)
            attention(BH)

        @block.tensor
        def _(pe):
            pe.sem_inc(S["pv"], PV0)
            pe.wait_ge(S["const_rdy"], 2)
            pe.wait_ge(S["init_rdy"], 1)
            with pe.Fori(0, B) as b:
                for u in range(2):
                    n = 2 * b + u
                    pe.wait_ge(S["xn_rdy"], n + 1)
                    pe.wait_ge(S["xnt_rdy"], ONE + n)
                    for t in range(GT):
                        last = pe.transpose(ps_t[:, t * P:(t + 1) * P], xs[:, u, t, :], ident)
                    last.then_inc(S["tr_rdy"], 1)
                    pe.wait_ge(S["xnt_rdy"], ONE + n + 1)
                    pe.wait_ge(S["v_rdy"], ONE + n)
                    pe.wait_ge(S["v_evac"], ONE + n)
                    pe.wait_ge(S["lg_rdy"], ONE + n)
                    pe.matmul(ps_qk[0:PROWS, :], wqk[:], xnt[:, u, :], start=True, stop=True)
                    for t in range(GT):
                        o = ps_v[:, t // 2, (t % 2) * 256:(t % 2) * 256 + C + E]
                        pe.matmul(o, xnt[:, u, t * P:(t + 1) * P], wvr[:], start=True, stop=False)
                        last = pe.matmul(o, ones1[:], bvr[:], start=False, stop=True)
                    last.then_inc(S["proj_rdy"], 1)
                    pe.wait_ge(S["hi_rdy"], n + 1)
                    pe.wait_ge(S["kmax_rdy"], ONE + b)
                    pe.matmul(ps_ku[:, u, :], cbf[KROW:KROW + QP, C_KDIR:C_KDIR + P], parts[KROW:KROW + QP, u, 0, :],
                              start=True, stop=True).then_inc(S["ku_rdy"], 1)
                for u in range(2):
                    n = 2 * b + u
                    pe.wait_ge(S["shift_rdy"], ONE + n)
                    pe.matmul(ps_p[:, 0, :], cbf[0:QP, C_PDIR:C_PDIR + P], parts[0:QP, u, 0, :], start=True, stop=True)
                    pe.matmul(ps_p[:, 1, :], cbf[0:QP, C_RDIR:C_RDIR + P], parts[0:QP, u, 0, :], start=True,
                              stop=True).then_inc(S["p_rdy"], 1)
                    pe.wait_ge(S["hat_rdy"], n + 1)
                    pe.matmul(ps_p[0:H, 0, :], cbf[:, C_BO:C_BO + H], hatm[:], start=True,
                              stop=True).then_inc(S["u_rdy"], 1)
            pe.wait_ge(S["cnt_rdy"], 1)
            for half in range(2):
                cols = slice(half * HALF, (half + 1) * HALF)
                pe.matmul(ps[:, half, :], cbf[:, C_TRI:C_TRI + P], cntb[:, 0:1024][:, cols], start=True, stop=False)
                last = pe.matmul(ps[:, half, :], onesb[:], cntb[:, 1024:2048][:, cols], start=False, stop=True)
            last.then_inc(S["pos_rdy"], 1)
            pe.wait_ge(S["route"], 1)
            def slot(b, j):
                before, jj = (b, j - RING) if j >= RING else (b - 1, NJ + j - RING)
                if not (isinstance(before, int) and before < 0):
                    if jj in UNIT_AT:
                        pe.wait_ge(S["exps"], NU * before + UNIT_AT[jj] + 1)
                    elif jj > NJ // NHG:
                        pe.wait_ge(S["att_rdy"], NHG * before + 1)
                    elif not (isinstance(before, int) and before < 1):
                        pe.wait_ge(S["att_rdy"], NHG * before)
                return ring[j % RING]

            def scores(b, n):
                hg, kc, g = n // NS, n % NS // HG, n % HG
                if n % NS == 0:
                    pe.wait_ge(S[f"ld{hg}"], NLOAD * (b + 1))
                s = slot(b, unit_job(n))
                for half in range(2):
                    last = pe.matmul(s[:, half, :], kz[:, hg, g, kc * P:(kc + 1) * P],
                                     q1[:, hg, half * HALF:(half + 1) * HALF], start=True, stop=True)
                last.then_inc(S["s1"], 1)

            def shifted(b, n):
                hg, kc, g = n // NS, n % NS // HG, n % HG
                pe.wait_ge(S["relu"], NU * b + n + 1)
                s = ring[unit_job(n) % RING]
                for half in range(2):
                    last = pe.matmul(s[:, half, :], kz[:, hg, g, kc * P:(kc + 1) * P],
                                     q2[:, hg, half * HALF:(half + 1) * HALF], start=False, stop=True,
                                     skip_group_check=True)
                last.then_inc(S["s2"], 1)

            def values(b, n):
                c, quarter = n // HG, n % HG
                hg, kc, half = c // TB, c % TB, quarter // 2
                if quarter == 0:
                    pe.wait_ge(S["exps"], NU * b + HG * (c + 1))
                if kc == 0:
                    pe.wait_ge(S["vp_rdy"], NHG * b + hg + 1)
                    m = 2 * NHG * b + 2 * hg - 1 + half
                    if not (isinstance(m, int) and m <= 0):
                        pe.wait_ge(S["acc_evac"], m)
                for g in range(HG):
                    last = pe.matmul(ps_acc[32 * g:32 * g + 32, half, quarter % 2 * QW:(quarter % 2 + 1) * QW],
                                     vp[:, hg, kc, g, :], pr[:, c % 2, g, quarter * QW:(quarter + 1) * QW],
                                     start=(kc == 0 and quarter % 2 == 0), stop=(kc == TB - 1 and quarter % 2 == 1),
                                     tile_position=(0, 32 * g), skip_group_check=True)
                last.then_inc(S["pv"], 1)

            def turn(b, hg, slot_of):
                pe.wait_ge(S["acc_evac"], 2 * (NHG * b + hg + 1))
                s = slot_of()
                for t in range(TB):
                    last = pe.transpose(s[:, t // 4, (t % 4) * P:(t % 4 + 1) * P], ot[:, t * P:(t + 1) * P], ident)
                last.then_inc(S["o_rdy"], 1)

            def sequence(b, first, last):
                for n in range(NU):
                    if n + 1 == TURN and not first:
                        turn(b - 1, 1, lambda: slot(b, unit_job(TURN) - 1))
                    if n + 1 == NS + TURN:
                        turn(b, 0, lambda: slot(b, unit_job(NS + TURN) - 1))
                    if n + 1 < NU:
                        scores(b, n + 1)
                    elif not last:
                        scores(b + 1, 0)
                    if n >= VLAG:
                        values(b, n - VLAG)
                    elif not first:
                        values(b - 1, NU + n - VLAG)
                    shifted(b, n)

            def attention(b0):
                scores(b0, 0)
                sequence(b0, True, False)
                with pe.Fori(b0 + 1, b0 + BH - 1) as b:
                    sequence(b, False, False)
                end = b0 + BH - 1
                sequence(end, False, True)
                for n in range(NU - VLAG, NU):
                    values(end, n)
                turn(end, 1, lambda: ring[TURN % RING])

            attention(0)
            pe.wait_ge(S["att_rdy"], NHG * BH)
            with pe.Fori(0, E_MLP // 2) as k:
                for u in range(2):
                    e = 2 * k + u
                    pe.wait_ge(S[f"ed{u}"], 80 * (k + 1))
                    for half in range(2):
                        for t in range(4):
                            j = half * 4 + t
                            last = pe.transpose(ps[:, half, t * P:(t + 1) * P], dd[:, u, j * P:(j + 1) * P], ident)
                        last.then_inc(S["etr"], 1)
                    pe.wait_ge(S["edt"], 2 * (e + 1))
                    pe.wait_ge(S["gel"], ONE + 8 * e)
                    for f in range(FC):
                        for half in range(2):
                            n = f * 2 + half
                            if n >= 4:
                                pe.wait_ge(S["gel"], ONE + 8 * e + n - 3)
                            pe.matmul(ps[:, 2 + n % 4, :], w1[:, 2 * u * FFN + f * P:2 * u * FFN + (f + 1) * P],
                                      dt_[:, half * HALF:(half + 1) * HALF], start=True, stop=True
                                      ).then_inc(S["fc1"], 1)
                    pe.wait_ge(S["gel"], ONE + 8 * (e + 1))
                    pe.wait_ge(S["yo_rdy"], ONE + e)
                    for j in range(ST):
                        o = ps[:, 6 + j // 4, (j % 4) * P:(j % 4 + 1) * P]
                        for f in range(FC):
                            last = pe.matmul(o, hs[:, f, j * P:(j + 1) * P],
                                             w1[:, (2 * u + 1) * FFN + f * P:(2 * u + 1) * FFN + (f + 1) * P],
                                             start=(f == 0), stop=(f == FC - 1))
                    last.then_inc(S["fc2"], 1)
            pe.wait_ge(S["gel"], ONE + 8 * E_MLP)
            pe.wait_ge(S["yo_rdy"], ONE + E_MLP)
            attention(BH)

        @block.vector
        def _(dve):
            step = [0]
            stat = S["bns"]

            def link(ins):
                step[0] += 1
                ins.then_inc(stat, 1)
                dve.wait_ge(stat, step[0])

            for name in FROM_ONE:
                dve.sem_inc(S[name], ONE)
            dve.sem_inc(S["lo_rdy"], LO0)
            dve.sem_inc(S["comb"], CO0)
            dve.memset(rowones[:], 1.0)
            dve.memset(kz[:].rearrange("p a b m -> p (a b m)").bitcast(F32), 0.0)
            dve.memset(q1[:].rearrange("p a m -> p (a m)").bitcast(F32), 0.0)
            dve.memset(q2[:].rearrange("p a m -> p (a m)").bitcast(F32), 0.0).then_inc(S["ztile"], 1)
            dve.memset(pr[:, 0, 3, :], 0.0).then_inc(S["ztile"], 1)
            dve.wait_ge(S["w_in"], 16 * 10)
            dve.tensor_copy(cbf[:], cst[:, 0:C_DESC]).then_inc(S["const_rdy"], 1)
            dve.tensor_scalar(wvr[:, C:C + E], wvr[:, C:C + E], nw[:, 0:1], None, ALU.mult
                              ).then_inc(S["const_rdy"], 1)
            dve.wait_ge(S["x_in"], 16 * B)
            with dve.Fori(0, B) as b:
                for t in range(TB):
                    last = dve.bn_stats(bst[:, bass.ds(b * TB + t, 1), :].rearrange("p a s -> p (a s)"),
                                        y[:, bass.ds(b * TB + t, 1), :].rearrange("p a c -> p (a c)"))
                last.then_inc(stat, 1)
            step[0] = B
            dve.wait_ge(stat, B)
            me, se, mo, so = (bst[:, :, k] for k in (1, 2, 4, 5))
            link(dve.tensor_tensor(mean, me, mo, ALU.add))
            link(dve.tensor_tensor(s6, me, mo, ALU.subtract))
            link(dve.tensor_tensor(var, se, so, ALU.add))
            link(dve.tensor_tensor(s6, s6, s6, ALU.mult))
            link(dve.tensor_scalar(mean, mean, 0.5, None, ALU.mult))
            link(dve.tensor_scalar(var, var, 1.0 / C, None, ALU.mult))
            link(dve.scalar_tensor_tensor(out=var, in0=s6, scalar=0.25, in1=var, op0=ALU.mult, op1=ALU.add))
            dve.tensor_scalar(s4, var, EPS, None, ALU.add).then_inc(S["stat_d"], 1)
            dve.wait_ge(S["stat_a"], 1)
            link(dve.reciprocal(rstd, rstd))
            link(dve.tensor_tensor(s7, var, rstd, ALU.mult))
            link(dve.tensor_tensor(s7, s7, rstd, ALU.mult))
            dve.tensor_scalar(s5, s7, EPS, None, ALU.add).then_inc(S["stat_d"], 1)
            dve.wait_ge(S["stat_a"], 2)
            dve.reciprocal(r2, r2).then_inc(S["stat_rdy"], 1)
            dve.wait_ge(S["stat_rdy"], 1)

            with dve.Fori(0, B) as b:
                for u in range(2):
                    n = 2 * b + u
                    tiles = bass.ds(b * TB + u * GT, GT)
                    dve.wait_ge(S["tr_rdy"], ONE + n)
                    dve.wait_ge(S["xn2_a"], ONE + n)
                    for t in range(GT):
                        tt = bass.ds(b * TB + u * GT + t, 1)
                        last = dve.tensor_scalar(xs[:, u, t, :], y[:, tt, :].rearrange("p a c -> p (a c)"),
                                                 mean[:, tt], rstd[:, tt], ALU.subtract, ALU.mult)
                    last.then_inc(S["xn_rdy"], 1)
                    dve.wait_ge(S["xn_rdy"], n + 1)
                    dve.tensor_tensor(y[:, tiles, :], y[:, tiles, :], xs[:, u, :, :], ALU.add).then_inc(S["y_upd"], 1)
                    dve.wait_ge(S["proj_rdy"], n + 1)
                    dve.wait_ge(S["lo_rdy"], n)
                    dve.tensor_scalar(v32[0:PROWS, u, :], ps_qk[0:PROWS, :], bqk[0:PROWS, 0:1],
                                      cst[0:PROWS, C_SCALE:C_SCALE + 1], ALU.add, ALU.mult).then_inc(S["v_rdy"], 1)
                    dve.wait_ge(S["v_evac"], ONE + n + 1)
                    dve.tensor_tensor(lg[:, tiles, :].rearrange("p (a t) e -> p a t e", a=2),
                                      ps_v.rearrange("p a (t c) -> p a t c", t=2)[:, :, :, C:C + E],
                                      r2[:, tiles].rearrange("p (a t) -> p a t", a=2).unsqueeze(3)
                                      .broadcast_to([P, 2, 2, E]), ALU.mult).then_inc(S["lg_rdy"], 1)
                dve.wait_ge(S["ku_rdy"], 2 * b + 2)
                dve.tensor_reduce(kmax[:], ps_ku, AX.XY, ALU.max).then_inc(S["kmax_rdy"], 1)
                dve.wait_ge(S["kmax_rdy"], ONE + b + 1)
                for u in range(2):
                    n = 2 * b + u
                    dve.wait_ge(S["hat1_rdy"], n + 1)
                    dve.tensor_tensor(hat[:], ps_p[:, 1, :], hat1[:], ALU.min).then_inc(S["hat_a"], 1)
                    dve.wait_ge(S["hat_a"], n + 1)
                    dve.tensor_scalar(hatm[:], hat[:], 0.0, kmax[:, 0:1], ALU.max, ALU.mult).then_inc(S["hat_rdy"], 1)
                    dve.wait_ge(S["ub_rdy"], n + 1)
                    dve.wait_ge(S[f"shift_out{u}"], ONE + 16 * b)
                    dve.scalar_tensor_tensor(out=shift[:, u, :], in0=ps_p[0:H, 0, :], scalar=-1.0 / SLOPE, in1=ub[:],
                                             op0=ALU.mult, op1=ALU.min).then_inc(S["shift_rdy"], 1)

            big3 = [big[:, k, :].rearrange("p (t e) -> p t e", e=E) for k in range(4)]
            b4 = pr[:, 1, 2, :].rearrange("p (t e) -> p t e", e=E)
            b5 = pr[:, 1, 3, :].rearrange("p (t e) -> p t e", e=E)
            sm = [small[:, k, :] for k in range(12)]

            def per_tile(v):
                return v.unsqueeze(2).broadcast_to([P, NT, E])

            descb = desc.unsqueeze(1).broadcast_to([P, NT, E])
            dve.wait_ge(S["zero_in"], 16 * E_MLP)
            for u in range(2):
                dve.wait_ge(S[f"parts_out{u}"], ONE + 64 * B)
            dve.wait_ge(S["lg_rdy"], ONE + 2 * B)
            link(dve.tensor_tensor(lg[:], lg[:], rb[:].unsqueeze(1).broadcast_to([P, NT, E]), ALU.add))
            link(dve.tensor_reduce(sm[0], lg[:], AX.X, ALU.max))
            dve.tensor_tensor(big3[0], lg[:], per_tile(sm[0]), ALU.subtract).then_inc(S["rpool"], 1)
            dve.wait_ge(S["r_exp"], 1)
            link(dve.tensor_reduce(sm[0], big3[1], AX.X, ALU.add))
            link(dve.reciprocal(sm[1], sm[0]))
            link(dve.tensor_tensor(big3[0], big3[1], per_tile(sm[1]), ALU.mult))
            for k, prob, onehot in ((0, big3[0], big3[2]), (1, big3[1], big3[3])):
                gate, rank = sm[2 + k], sm[4 + k]
                if k:
                    link(dve.scalar_tensor_tensor(out=prob, in0=big3[2], scalar=-2.0, in1=big3[0], op0=ALU.mult,
                                                  op1=ALU.add))
                link(dve.tensor_reduce(gate, prob, AX.X, ALU.max))
                link(dve.tensor_tensor(b4, prob, per_tile(gate), ALU.is_equal))
                link(dve.tensor_tensor(b4, b4, descb, ALU.mult))
                link(dve.tensor_reduce(rank, b4, AX.X, ALU.max))
                link(dve.tensor_tensor(onehot, b4, per_tile(rank), ALU.is_equal))
            cnt = pr[:, 1, 2, :].rearrange("p (e t) -> p e t", t=NT)
            incl = pr[:, 1, 3, :]
            reset = big[:, 0, :]
            link(dve.tensor_tensor(cnt.rearrange("p e t -> p t e"), big3[2], big3[3], ALU.add))
            link(dve.memset(reset, 1.0))
            link(dve.memset(reset.rearrange("p (e t) -> p e t", t=NT)[:, :, 0:1], 0.0))
            link(dve.tensor_tensor_scan(incl, reset, pr[:, 1, 2, :], 0.0, ALU.mult, ALU.add))
            link(dve.tensor_copy(cntb[:, 0:1024], pr[:, 1, 2, :]))
            dve.tensor_tensor(cntb[:, 1024:2048], incl, pr[:, 1, 2, :], ALU.subtract).then_inc(S["cnt_rdy"], 1)
            dve.wait_ge(S["pos_rdy"], 1)
            pos = ps[:, 0:2, :].rearrange("p a m -> p (a m)").rearrange("p (e t) -> p t e", t=NT)
            for k in range(2):
                onehot, gate, rank, at, keep = big3[2 + k], sm[2 + k], sm[4 + k], sm[6 + k], sm[8 + k]
                link(dve.tensor_tensor(b5, pos, onehot, ALU.mult))
                link(dve.tensor_reduce(at, b5, AX.X, ALU.add))
                link(dve.tensor_scalar(keep, at, float(CAP), None, ALU.is_lt))
                link(dve.tensor_tensor(gate, gate, keep, ALU.mult))
            link(dve.tensor_tensor(sm[0], sm[2], sm[3], ALU.add))
            link(dve.tensor_scalar(sm[1], sm[0], 0.0, None, ALU.is_le))
            link(dve.tensor_tensor(sm[0], sm[0], sm[1], ALU.add))
            link(dve.reciprocal(sm[0], sm[0]))
            for k in range(2):
                gate, rank, at, keep = sm[2 + k], sm[4 + k], sm[6 + k], sm[8 + k]
                link(dve.tensor_tensor(gate, gate, sm[0], ALU.mult))
                link(dve.scalar_tensor_tensor(out=keep, in0=rank, scalar=float(E_MLP), in1=keep, op0=ALU.is_le,
                                              op1=ALU.mult))
                link(dve.tensor_tensor(co[:, k, :], gate, keep, ALU.mult))
                link(dve.scalar_tensor_tensor(out=at, in0=rank, scalar=-float(CAP), in1=at, op0=ALU.mult, op1=ALU.add))
                link(dve.tensor_scalar(sm[10], keep, -SKIP, SKIP + SLOTS, ALU.mult, ALU.add))
                link(dve.tensor_tensor(at, at, sm[10], ALU.add))
                link(dve.tensor_copy(idx[:, k, :], at))
            for n in range(3):
                r = float(E - 1 - n)
                link(dve.scalar_tensor_tensor(out=sm[10], in0=sm[4], scalar=r, in1=sm[2], op0=ALU.is_equal,
                                              op1=ALU.mult))
                link(dve.scalar_tensor_tensor(out=sm[11], in0=sm[5], scalar=r, in1=sm[3], op0=ALU.is_equal,
                                              op1=ALU.mult))
                last = dve.tensor_tensor(co[:, 2 + n, :], sm[10], sm[11], ALU.add)
                if n < 2:
                    link(last)
            last.then_inc(S["route"], 1)
            dve.wait_ge(S["route"], 1)


            def finish(b, hg, j):
                m = NHG * b + hg
                dve.wait_ge(S["o_rdy"], m + 1)
                o3 = ring[j % RING].rearrange("p a (t g c) -> p (a t) g c", g=HG, c=32)
                dve.reciprocal(rg[:], o3[:, :, :, DV]).then_inc(S["rg_rdy"], 1)
                dve.wait_ge(S["rg_rdy"], 2 * m + 1)
                dve.tensor_scalar(rg[:], rg[:], gam[:, 0:1], None, ALU.mult).then_inc(S["rg_rdy"], 1)
                dve.wait_ge(S["rg_rdy"], 2 * m + 2)
                if not (isinstance(m, int) and m == 0):
                    dve.wait_ge(S["y_att"], m)
                dve.tensor_tensor(att[:], o3[:, :, :, 0:DV], rg[:].unsqueeze(3).broadcast_to([P, TB, HG, DV]),
                                  ALU.mult).then_inc(S["att_rdy"], 1)

            def combine(k, i):
                n = 2 * TB * k + i
                tt = bass.ds(n, 1)
                yt = y[:, tt, :].rearrange("p a c -> p (a c)")
                dve.wait_ge(S[f"gath{i % 4}"], 32 * (2 * TB // 4 * k + i // 4 + 1))
                dve.scalar_tensor_tensor(out=yt, in0=g1[:, i % 4, 0, :], scalar=co[:, 0, tt], in1=yt, op0=ALU.mult,
                                         op1=ALU.add).then_inc(S["first_row"], 1)
                dve.wait_ge(S["first_row"], n + 1)
                dve.scalar_tensor_tensor(out=yt, in0=g1[:, i % 4, 1, :], scalar=co[:, 1, tt], in1=yt, op0=ALU.mult,
                                         op1=ALU.add).then_inc(S["comb"], 1)

            def sequence(b, first, k=None):
                for n in range(NU):
                    if k is not None and n >= COMB0 and (n - COMB0) % COMBS == 0 and (n - COMB0) // COMBS < 2 * TB:
                        combine(k, (n - COMB0) // COMBS)
                    if n == TURN and not first:
                        finish(b - 1, 1, unit_job(TURN) - 1)
                    if n == NS + TURN:
                        finish(b, 0, unit_job(NS + TURN) - 1)
                    dve.wait_ge(S["s1"], NU * b + n + 1)
                    s = ring[unit_job(n) % RING].rearrange("p a m -> p (a m)")
                    dve.tensor_scalar(s, s, 0.0, 1.0 / SLOPE - 1.0, ALU.max, ALU.mult).then_inc(S["relu"], 1)

            sequence(0, True)
            with dve.Fori(1, BH) as b:
                sequence(b, False)
            finish(BH - 1, 1, TURN)

            with dve.Fori(0, E_MLP // 2) as k:
                for u in range(2):
                    e = 2 * k + u
                    dve.wait_ge(S["fc2"], e + 1)
                    dve.wait_ge(S["yo_out"], ONE + 16 * e)
                    dve.tensor_tensor(yo.rearrange("p (j c) -> p j c", c=C),
                                      ps[:, 6:8, :].rearrange("p a (j c) -> p (a j) c", c=C),
                                      b2s[:, u, :].unsqueeze(1).broadcast_to([P, ST, C]), ALU.add
                                      ).then_inc(S["yo_rdy"], 1)
            dve.memset(w1, 0.0).then_inc(S["ztile"], 1)
            dve.wait_ge(S["pool_step"], 6 * B)
            sequence(BH, True, 0)
            with dve.Fori(1, BH) as k:
                sequence(k + BH, False, k)
            finish(B - 1, 1, TURN)


_INS = ("x", "consts", "w_qk", "b_qk", "w_vr", "b_v", "r_b", "n_w", "n_w_row", "w1t", "b1", "w2t", "b2", "cvec",
        "gamma")


def layouts(i):
    import numpy as np

    a = {k.split("_", 1)[1]: np.asarray(v) for k, v in i.items()}
    q, k = ({n: a[f"attn_{n}{w}"].reshape(H, DQ, -1).transpose(1, 0, 2).reshape(QP, -1) for n in "Wb"} for w in "qk")
    rows = {}
    for n, width in (("W", C), ("b", 1)):
        r = np.zeros((PROWS, width), np.float32)
        r[0:3 * QP] = np.tile(q[n], (3, 1))
        r[KROW:] = np.tile(k[n], (3, 1))
        rows[n] = r
    return {
        "x": a["attn_x"].reshape(T, C),
        "consts": constants(),
        "w_qk": rows["W"].T,
        "b_qk": rows["b"],
        "w_vr": np.concatenate([a["attn_Wv"].T, a["ffn_router_weight"].T], axis=1),
        "b_v": a["attn_bv"].reshape(1, C),
        "r_b": a["ffn_router_bias"].reshape(1, E),
        "n_w": a["ffn_norm_weight"].reshape(C, 1),
        "n_w_row": a["ffn_norm_weight"].reshape(1, C),
        "w1t": a["ffn_fc1_weight"].transpose(0, 2, 1),
        "b1": a["ffn_fc1_bias"].reshape(E_MLP, FC, P).transpose(0, 2, 1),
        "w2t": a["ffn_fc2_weight"].transpose(0, 2, 1).reshape(E_MLP, FC, P, C).transpose(0, 2, 1, 3).reshape(E_MLP, P, FC * C),
        "b2": a["ffn_fc2_bias"],
        "cvec": a["ffn_constant_vectors"].reshape(1, 2, C),
        "gamma": a["attn_gamma"].reshape(1, 1),
    }


def kernel(**inputs):
    import numpy as np
    import concourse.bacc as bacc
    from concourse.bass_utils import run_bass_kernel_spmd

    nc = bacc.Bacc("TRN2", target_bir_lowering=False, num_devices=1)
    arrays, args = {}, []
    laid = layouts(inputs)
    for name in _INS:
        v = np.ascontiguousarray(laid[name])
        arrays[f"in_{name}"] = v
        args.append(nc.dram_tensor(f"in_{name}", v.shape, mybir.dt.from_np(v.dtype), kind="ExternalInput").ap())
    out = nc.dram_tensor("out", [T, C], F32, kind="ExternalOutput").ap()
    build(nc, *args, out)
    r = run_bass_kernel_spmd(nc, [arrays], core_ids=[0])
    return r.results[0]["out"].reshape(B, M, C)
```

```python
from contextlib import ExitStack

import concourse.bass as bass
from concourse import mybir

F32 = mybir.dt.float32
BF16 = mybir.dt.bfloat16
I32 = mybir.dt.int32
ALU = mybir.AluOpType
ACT = mybir.ActivationFunctionType
AX = mybir.AxisListType

P = 128
B, M, C = 8, 1024, 128
T = B * M
NT = T // P
TB = M // P
H, DV, DQ = 8, 16, 2
HG = 4
NHG = H // HG
GT = 4
LAGS = 6
GW = GT * P
HALF = 512
QP = H * DQ
KROW = 64
PROWS = KROW + 3 * QP
NPROD = 3 * 3 * DQ
NROW = NPROD + 1
DIRS = 16
E, E_MLP, FFN = 16, 12, 512
FC = FFN // P
CAP = T * 2 // E
SLOTS = E_MLP * CAP
ST = CAP // P
SKIP = float(1 << 20)
EPS = 1e-5
SLOPE = 0.2

BH = B // 2
NS = TB * HG
NU = NHG * NS
NJ = NU + NHG
RING = 3
GB = 2
VLAG = 5
TURN = 8

C_ID, C_TRI, C_KDIR, C_PDIR, C_RDIR, C_BO = 0, 128, 256, 384, 512, 640
C_DESC, C_SCALE, NCONST = 648, 664, 665


def constants():
    import math

    import numpy as np

    c = np.zeros((P, NCONST), np.float32)
    c[:, C_ID:C_ID + P] = np.eye(P)
    c[:, C_TRI:C_TRI + P] = -np.tril(np.ones((P, P)))
    step = 2 * math.pi / DIRS
    for j in range(DIRS):
        u = np.array([math.cos(j * step), math.sin(j * step)])
        before = np.array([math.cos((j - 1) * step), math.sin((j - 1) * step)])
        after = np.array([math.cos((j + 1) * step), math.sin((j + 1) * step)])
        p = np.array([-before[1], before[0]])
        r = np.array([-after[1], after[0]])
        p, r = p / (p @ u), r / (r @ u)
        for h in range(H):
            for d in range(DQ):
                row, col = d * H + h, h * DIRS + j
                c[KROW + row, C_KDIR + col] = u[d]
                c[row, C_PDIR + col] = p[d]
                c[row, C_RDIR + col] = r[d]
            c[h * DIRS + j, C_BO + h] = 1.0
    c[:, C_DESC:C_DESC + E] = E - np.arange(E)
    c[:, C_SCALE] = 1.0
    c[KROW:, C_SCALE] = 1.0 / math.sqrt(DQ)
    return c


def build(nc, x, consts, w_qk, b_qk, w_vr, b_v, r_b, n_w, n_w_row, w1t, b1, w2t, b2, cvec, gamma, out):
    parts_dram = nc.dram_tensor("parts_dram", [2, NROW * H, T], BF16, kind="Internal").ap()
    disp = nc.dram_tensor("disp", [SLOTS, C], F32, kind="Internal").ap()
    eout = nc.dram_tensor("eout", [SLOTS, C], F32, kind="Internal").ap()

    with ExitStack() as ctx:
        def sb(name, shape, dt=F32):
            return ctx.enter_context(nc.sbuf_tensor(name, shape, dt))

        def sem(name):
            return ctx.enter_context(nc.semaphore(name))

        y = sb("y", [P, NT, C])
        xn2 = sb("xn2", [P, NT, C])
        va = sb("va", [P, NT, H, DV + 1])
        cst = sb("cst", [P, NCONST])
        ident = cst[:, C_ID:C_ID + P]
        cbf = sb("cbf", [P, C_SCALE], BF16)
        wqk = sb("wqk", [P, PROWS])
        bqk = sb("bqk", [P, 1])
        wvr = sb("wvr", [P, C + E])
        bvg = sb("bvg", [P, C])
        rb = sb("rb", [P, E])
        nw = sb("nw", [P, 1])
        nwr = sb("nwr", [P, C])
        gam = sb("gam", [P, 1])
        cv = sb("cv", [P, 2, C])
        b1s = sb("b1s", [P, 2, FC])
        onesb = sb("onesb", [P, P], BF16)
        bst = sb("bst", [P, NT, 6])
        st = sb("st", [P, 8, NT])
        (mean, var, rstd, r2, s4, s5, s6, s7) = (st[:, k, :] for k in range(8))
        xs = sb("xs", [P, 2, GT, C])
        parts = sb("parts", [P, 2, 3, GW], BF16)
        hat1 = sb("hat1", [P, GW], BF16)
        hat = sb("hat", [P, 2, GW], BF16)
        kmax2 = sb("kmax2", [P, 2])
        kmax = sb("kmax", [P, 1])
        ub = sb("ub", [H, GW])
        shift = sb("shift", [H, 2, GW], BF16)
        kz = sb("kz", [P, NHG, HG, M], BF16)
        q1 = sb("q1", [P, NHG, M], BF16)
        q2 = sb("q2", [P, NHG, M], BF16)
        vp = sb("vp", [P, NHG, TB, HG, 32])
        pr = sb("pr", [P, 2, HG, M])
        ot = sb("ot", [P, M])
        rg = sb("rg", [P, TB, HG])
        att = sb("att", [P, TB, HG, DV])
        rowones = sb("rowones", [1, M], BF16)
        xnt, v32 = (pr[:, 1, k, :].rearrange("p (u m) -> p u m", u=2) for k in range(2))
        hatm = att[:].rearrange("p t g d -> p (t g d)").bitcast(BF16).rearrange("p (u m) -> p u m", u=2)
        rem = ot[:].rearrange("p (u m) -> p u m", u=2)
        lg = sb("lg", [P, NT, E])
        idx = sb("idx", [P, 2, NT], I32)
        idxs = sb("idxs", [P, 2, TB], I32)
        co = sb("co", [P, 5, NT])
        pflat = parts[:].rearrange("p u k m -> p (u k m)").bitcast(F32)
        rt = [pr[:, k // HG, k % HG, :] for k in range(2 * HG)]
        lg_off, ex = rt[0], rt[1]
        rbf = [rt[k // 2].bitcast(BF16)[:, (k % 2) * NT * E:(k % 2 + 1) * NT * E] for k in range(4 * HG)]
        oh1, oh2, rank_of, reset, cnt, incl = rbf[4:10]
        prod = rt[5], rt[6]
        small = rt[7].rearrange("p (k t) -> p k t", t=NT)
        top, total, inv, total2 = (small[:, k, :] for k in range(4))
        gate, rank, at, keep, tmp = (small[:, k:k + 2, :] for k in (4, 6, 8, 10, 12))
        rank_b = small[:, 14, :].bitcast(BF16).rearrange("p (k t) -> p k t", k=2)
        w1 = kz[:, 1, :, :].rearrange("p g m -> p (g m)").bitcast(F32)
        ef = pr[:, :, :, :].rearrange("p a b m -> p (a b) m")
        hs, dt_, yo = ef[:, 0:4, :], ef[:, 4, :], ef[:, 7, :]
        dd = [xs[:].rearrange("p u t c -> p (u t c)"), ef[:, 5, :]]
        b2s = pflat[:, 0:2 * C].rearrange("p (u c) -> p u c", c=C)
        g1 = xs[:].rearrange("p u (t k) c -> p u t k c", k=2)

        ps = ctx.enter_context(nc.psum_tensor("ps", [P, 8, HALF], F32))
        ps_t, ps_qk, ps_v, ps_p = ps[:, 0, :], ps[:, 1, :], ps[:, 2:4, :], ps[:, 6:8, :]
        ps_ku, ps_u = ps[:, 4, :], ps[0:H, 5, :]
        ring = [ps[:, 2 * k:2 * k + 2, :] for k in range(RING)]
        ps_acc = ps[:, 6:8, :]

        names = ("x_in0 x_in1 x_in2 x_in3 x_in4 x_in5 x_in6 x_in7 w_in zero_in const_rdy bns stat_d stat_a stat_rdy "
                 "xn_rdy tr_rdy xnt_rdy qk_rdy proj_rdy "
                 "v_rdy y_upd hi_rdy rem_rdy mid_rdy lo_rdy xn2_rdy v_evac lg_rdy parts_out0 parts_out1 dir_rdy ext_rdy "
                 "kmax_rdy hat1_rdy hat_rdy hatm_rdy u_rdy ub_rdy shift_rdy shift_out0 shift_out1 "
                 "weighted gate_rdy row_step route max_rdy off_rdy reset_rdy r_exp cnt_rdy pos_rdy ztile init_rdy kz_init "
                 "ld0 ld1 vp_rdy s1 relu s2 exps pv acc_evac o_rdy rg_rdy att_rdy y_att "
                 "scat staged pool_step carry "
                 "ed0 ed1 etr edt fc1 gel fc2 yo_rdy yo_out gath0 gath1 comb final").split()
        S = {n: sem(n) for n in names}

        block = ctx.enter_context(nc.Block())
        DV1 = DV + 1
        NLOAD = 16 * 3 * HG
        GS = 2 * NT

        def wait_done(engine, name, count):
            if not (isinstance(count, int) and count <= 0):
                engine.wait_ge(S[name], count)

        def groups(engine, step, meanwhile={}):
            def locate(b, u):
                def at(lag):
                    before, v = (lag - u + 1) // 2, (u - lag) % 2
                    if isinstance(b, int) and not 0 <= 2 * b + u - lag < 2 * B:
                        return None
                    return b - before, v, 2 * (b - before) + v
                return at

            for n in range(LAGS):
                step(locate(n // 2, n % 2))
            with engine.Fori(LAGS // 2, B) as b:
                for u in range(2):
                    step(locate(b, u))
            for n in range(LAGS):
                step(locate(B + n // 2, n % 2))
                if n in meanwhile:
                    meanwhile[n]()

        def unit_job(n):
            return n + (n >= TURN) + (n >= NS + TURN)

        UNIT_AT = {unit_job(n): n for n in range(NU)}
        ONE = 1
        FROM_ONE = ("gel", "yo_rdy", "yo_out")
        PV0 = NU
        CO0 = 2


        @block.sync
        def _(sp):
            for b in range(B):
                sp.dma_start(y[:, bass.ts(b, TB), :],
                             x[bass.ts(b, M), :].rearrange("(t p) c -> p t c", p=P)).then_inc(S[f"x_in{b}"], 16)
            for dst, src in ((cst[:], consts), (wqk[:], w_qk), (bqk[0:PROWS, :], b_qk), (wvr[:], w_vr),
                             (bvg[:], b_v.partition_broadcast(P)), (rb[:], r_b.partition_broadcast(P)), (nw[:], n_w),
                             (nwr[:], n_w_row.partition_broadcast(P)), (gam[:], gamma.partition_broadcast(P)),
                             (cv[:], cvec.partition_broadcast(P))):
                sp.dma_start(dst, src).then_inc(S["w_in"], 16)
            sp.wait_ge(S["init_rdy"], 1)
            sp.wait_ge(S["ztile"], 1)
            for hg in range(NHG):
                for g in range(HG):
                    r = 32 * g + NPROD
                    sp.dma_start(kz[r:r + 1, hg, g, :], rowones[:]).then_inc(S["kz_init"], 16)
            for e in range(E_MLP):
                sp.dma_start(disp[e * CAP:(e + 1) * CAP, :].rearrange("(p j) c -> p (j c)", p=P),
                             pr[:, 0, 3, :]).then_inc(S["zero_in"], 16)

            def store_parts(at):
                if at(0):
                    b, u, n = at(0)
                    cols = bass.ds(b * M + u * GW, GW)
                    sp.wait_ge(S["lo_rdy"], n + 1)
                    sp.dma_start(parts_dram[0, 0:NPROD * H, cols].rearrange("(i p) t -> p i t", i=3),
                                 parts[0:3 * QP, u, :, :]).then_inc(S[f"parts_out{u}"], 16)
                    for i in range(3):
                        r = i * 3 * QP
                        sp.dma_start(parts_dram[1, r:r + 3 * QP, cols].rearrange("(x p) t -> p x t", x=3),
                                     parts[KROW + i * QP:KROW + (i + 1) * QP, u, :, :]).then_inc(S[f"parts_out{u}"], 16)
                if at(5):
                    b, u, n = at(5)
                    sp.wait_ge(S["shift_rdy"], n + 1)
                    sp.dma_start(parts_dram[0, NPROD * H:NROW * H, bass.ds(b * M + u * GW, GW)],
                                 shift[:, u, :]).then_inc(S[f"shift_out{u}"], 16)

            groups(sp, store_parts)
            for u in range(2):
                sp.wait_ge(S[f"parts_out{u}"], 64 * B)
                sp.wait_ge(S[f"shift_out{u}"], 16 * B)
            sp.wait_ge(S["kz_init"], 16 * NHG * HG)

            def load_operands(b, hg):
                sp.wait_ge(S["pv"], NU * b + (hg + 1) * NS)
                for g in range(HG):
                    h = hg * HG + g
                    tok = bass.ts(b, M)
                    krows = parts_dram[1, :, tok].rearrange("(r h) t -> h r t", h=H)[h]
                    qrows = parts_dram[0, :, tok].rearrange("(r h) t -> h r t", h=H)[h]
                    r = 32 * g
                    sp.dma_start(kz[r:r + NPROD, hg, g, :], krows[0:NPROD, :]).then_inc(S[f"ld{hg}"], 16)
                    sp.dma_start(q1[r:r + NPROD, hg, :], qrows[0:NPROD, :]).then_inc(S[f"ld{hg}"], 16)
                    sp.dma_start(q2[r:r + NROW, hg, :], qrows).then_inc(S[f"ld{hg}"], 16)

            def store_sequence(s):
                sp.wait_ge(S["comb"], CO0 + TB // GB * (s + 1))
                sp.sem_inc(S["carry"], 1)
                sp.wait_ge(S["y_att"], NHG * (s + 1))
                sp.dma_start(out[bass.ts(s, M), :].rearrange("(t p) c -> p t c", p=P),
                             y[:, bass.ts(s, TB), :]).then_inc(S["final"], 16)

            with sp.Fori(0, BH) as b:
                for hg in range(NHG):
                    load_operands(b, hg)
            load_operands(BH, 0)
            sp.wait_ge(S["s2"], 2 * NU * BH)
            sp.wait_ge(S["scat"], 16 * GS)

            def load_expert(e, u):
                for dst, src in ((w1[:, (2 * u) * FFN:(2 * u + 1) * FFN], w1t[bass.ds(e, 1), :, :].rearrange("a p f -> p (a f)")),
                                 (w1[:, (2 * u + 1) * FFN:(2 * u + 2) * FFN], w2t[bass.ds(e, 1), :, :].rearrange("a p f -> p (a f)")),
                                 (b1s[:, u, :], b1[bass.ds(e, 1), :, :].rearrange("a p f -> p (a f)")),
                                 (b2s[:, u, :], b2[bass.ds(e, 1), :].partition_broadcast(P)),
                                 (dd[u], disp[bass.ds(e * CAP, CAP), :].rearrange("(p j) c -> p (j c)", p=P))):
                    sp.dma_start(dst, src).then_inc(S[f"ed{u}"], 16)

            def store_expert(e):
                sp.wait_ge(S["yo_rdy"], ONE + e + 1)
                sp.dma_start(eout[bass.ds(e * CAP, CAP), :].rearrange("(p j) c -> p (j c)", p=P),
                             yo).then_inc(S["yo_out"], 16)

            load_expert(0, 0)
            sp.wait_ge(S["pv"], PV0 + NU * BH)
            load_expert(1, 1)
            with sp.Fori(0, E_MLP // 2 - 1) as k:
                for u in range(2):
                    store_expert(2 * k + u)
                    load_expert(2 * k + u + 2, u)
            for u in range(2):
                store_expert(E_MLP - 2 + u)
            sp.wait_ge(S["ztile"], 2)
            for g in range(HG):
                r = 32 * g + NPROD
                sp.dma_start(kz[r:r + 1, 1, g, :], rowones[:]).then_inc(S["kz_init"], 16)
            sp.wait_ge(S["kz_init"], 16 * (NHG + 1) * HG)
            load_operands(BH, 1)
            with sp.Fori(1, BH) as k:
                for hg in range(NHG):
                    load_operands(k + BH, hg)
                for u in range(2):
                    store_sequence(2 * k - 2 + u)
            for u in range(2):
                store_sequence(B - 2 + u)
            sp.wait_ge(S["final"], 16 * B)

        @block.gpsimd
        def _(pool):
            pool.memset(onesb[:], 1.0)
            pool.memset(pr[:, 0, 3, :], 0.0).then_inc(S["ztile"], 1)
            pool.memset(rowones[:], 1.0)
            for a in (kz[:].rearrange("p a b m -> p (a b m)"), q1[:].rearrange("p a m -> p (a m)"),
                      q2[:].rearrange("p a m -> p (a m)")):
                pool.memset(a.bitcast(F32), 0.0)
            pool.memset(va[:, :, :, DV:DV1], 1.0)
            pool.memset(vp[:], 0.0).then_inc(S["init_rdy"], 1)

            def prologue(at):
                if at(1):
                    b, u, n = at(1)
                    pool.wait_ge(S["hi_rdy"], n + 1)
                    wait_done(pool, "lo_rdy", n - 1)
                    pool.tensor_tensor(rem[0:PROWS, u, :], v32[0:PROWS, u, :], parts[0:PROWS, u, 0, :],
                                       ALU.subtract).then_inc(S["rem_rdy"], 1)
                if at(0):
                    b, u, n = at(0)
                    tiles = bass.ds(b * TB + u * GT, GT)
                    pool.wait_ge(S["xn_rdy"], n + 1)
                    pool.sem_inc(S["carry"], 1)
                    pool.tensor_tensor(y[:, tiles, :], y[:, tiles, :], xs[:, u, :, :], ALU.add).then_inc(S["y_upd"], 1)
                if at(1):
                    b, u, n = at(1)
                    pool.wait_ge(S["mid_rdy"], n + 1)
                    pool.tensor_tensor(parts[0:PROWS, u, 2, :], rem[0:PROWS, u, :], parts[0:PROWS, u, 1, :],
                                       ALU.subtract).then_inc(S["lo_rdy"], 1)

            groups(pool, prologue)
            pool.wait_ge(S["zero_in"], 16 * E_MLP)
            restarts = reset.rearrange("p (e t) -> p e t", t=NT)
            pool.memset(restarts[:, :, 1:NT], 1.0)
            pool.memset(restarts[:, :, 0:1], 0.0).then_inc(S["reset_rdy"], 1)
            pool.wait_ge(S["max_rdy"], 1)
            pool.tensor_tensor(lg_off.rearrange("p (t e) -> p t e", e=E), lg[:],
                               top.unsqueeze(2).broadcast_to([P, NT, E]), ALU.subtract
                               ).then_inc(S["off_rdy"], 1)
            pool.wait_ge(S["v_evac"], 2 * B)
            pool.wait_ge(S["xn2_rdy"], 2 * B)
            pool.wait_ge(S["zero_in"], 16 * E_MLP)

            def value_rows(b, hg):
                pool.wait_ge(S["pv"], NU * b + (hg + 1) * NS)
                pool.tensor_copy(vp[:, hg, :, :, 0:DV1],
                                 va[:, bass.ts(b, TB), hg * HG:(hg + 1) * HG, :]).then_inc(S["vp_rdy"], 1)

            def add_attention(b, hg):
                pool.wait_ge(S["att_rdy"], NHG * b + hg + 1)
                pool.sem_inc(S["carry"], 1)
                ys = y[:, bass.ts(b, TB), hg * HG * DV:(hg + 1) * HG * DV]
                pool.tensor_tensor(ys, ys, att[:, :, :, :].rearrange("p t g d -> p t (g d)"),
                                   ALU.add).then_inc(S["y_att"], 1)

            def stage(s, count):
                pool.tensor_copy(idxs[:], idx[:, :, bass.ds(s * TB, TB)]).then_inc(S["staged"], 1)
                pool.wait_ge(S["staged"], count)
                pool.sem_inc(S["carry"], 1)

            def scatter(s):
                pool.tensor_copy(xs[:].rearrange("p u t c -> p (u t) c"), xn2[:, bass.ds(s * TB, TB), :])
                stage(s, s + 1)
                for t in range(TB):
                    for k in range(2):
                        pool.indirect_dma_start(
                            out=disp, out_offset=bass.IndirectOffsetOnAxis(ap=idxs[:, k, t:t + 1], axis=0),
                            in_=xs[:, t // GT, t % GT, :], in_offset=None,
                            bounds_check=SLOTS - 1, oob_is_err=False).then_inc(S["scat"], 16)
                pool.wait_ge(S["scat"], 16 * 2 * TB * (s + 1))

            def gather(s):
                stage(s, B + s + 1)

                def fetch(i):
                    pool.wait_ge(S["comb"], TB // GB * s + i + 1)
                    pool.sem_inc(S["carry"], 1)
                    for t in range(GB):
                        for c in range(2):
                            pool.indirect_dma_start(
                                out=g1[:, i % 2, t, c, :], out_offset=None, in_=eout,
                                in_offset=bass.IndirectOffsetOnAxis(ap=idxs[:, c, GB * i + t:GB * i + t + 1], axis=0),
                                bounds_check=SLOTS - 1, oob_is_err=False).then_inc(S[f"gath{i % 2}"], 16)

                def combine(i):
                    g = g1[:, i % 2, :, :, :]
                    tiles = bass.ds(s * TB + GB * i, GB)
                    yt = y[:, tiles, :]
                    pool.wait_ge(S[f"gath{i % 2}"], 32 * GB * (TB // GB // 2 * s + i // 2 + 1))
                    pool.sem_inc(S["carry"], 1)
                    for c in range(2):
                        last = pool.tensor_tensor(g[:, :, c, :], g[:, :, c, :],
                                                  co[:, c, tiles].unsqueeze(2).broadcast_to([P, GB, C]), ALU.mult)
                    last.then_inc(S["weighted"], 1)
                    for c in range(2):
                        pool.wait_ge(S["weighted"], 2 * (TB // GB * s + i) + 1 + c)
                        pool.sem_inc(S["carry"], 1)
                        pool.tensor_tensor(yt, yt, g[:, :, c, :], ALU.add).then_inc(S["comb" if c else "weighted"], 1)

                for i in range(TB // GB):
                    fetch(i)
                    if i > 0:
                        combine(i - 1)
                combine(TB // GB - 1)

            def sequence(b, move, k, last):
                value_rows(b, 1)
                for u in range(2):
                    move(2 * k + u)
                if not last:
                    value_rows(b + 1, 0)
                if move is gather:
                    pool.wait_ge(S["comb"], CO0 + 2 * TB // GB * (k + 1))
                add_attention(b, 0)
                add_attention(b, 1)

            value_rows(0, 0)
            count = 0

            def link(ins):
                nonlocal count
                count += 1
                ins.then_inc(S["row_step"], 1)
                pool.wait_ge(S["row_step"], count)

            pool.wait_ge(S["gate_rdy"], 1)
            link(pool.tensor_scalar(tmp, rank, float(E_MLP), None, ALU.is_le))
            link(pool.tensor_tensor(keep, keep, tmp, ALU.mult))
            link(pool.tensor_tensor(co[:, 0:2, :], gate, keep, ALU.mult))
            link(pool.tensor_scalar(tmp, rank, -float(CAP), None, ALU.mult))
            link(pool.tensor_tensor(at, at, tmp, ALU.add))
            link(pool.tensor_scalar(tmp, keep, -SKIP, SKIP + SLOTS, ALU.mult, ALU.add))
            link(pool.tensor_tensor(at, at, tmp, ALU.add))
            link(pool.tensor_copy(idx[:], at))
            for n in range(3):
                link(pool.tensor_scalar(tmp, rank, float(E - 1 - n), None, ALU.is_equal))
                link(pool.tensor_tensor(tmp, tmp, gate, ALU.mult))
                link(pool.tensor_tensor(co[:, 2 + n, :], tmp[:, 0, :], tmp[:, 1, :], ALU.add))
            pool.sem_inc(S["route"], 1)
            with pool.Fori(0, BH - 1) as b:
                sequence(b, scatter, b, False)
            sequence(BH - 1, scatter, BH - 1, True)
            value_rows(BH, 0)
            with pool.Fori(0, B) as b:
                tiles = bass.ds(b * TB, TB)
                pool.wait_ge(S["scat"], 16 * GS)
                xb, yb = xn2[:, tiles, :], y[:, tiles, :]

                for k in range(3):
                    weight = co[:, 2 + k, tiles].unsqueeze(2).broadcast_to([P, TB, C])
                    what = xb if k == 0 else cv[:, k - 1, :].unsqueeze(1).broadcast_to([P, TB, C])
                    pool.tensor_tensor(xb, what, weight, ALU.mult).then_inc(S["pool_step"], 1)
                    pool.wait_ge(S["pool_step"], 7 * b + 2 * k + 1)
                    pool.sem_inc(S["carry"], 1)
                    pool.tensor_tensor(yb, yb, xb, ALU.add).then_inc(S["pool_step"], 1)
                    pool.wait_ge(S["pool_step"], 7 * b + 2 * k + 2)
                    pool.sem_inc(S["carry"], 1)
                pool.tensor_tensor(yb, yb, bvg[:].unsqueeze(1).broadcast_to([P, TB, C]), ALU.add
                                   ).then_inc(S["pool_step"], 1)
            pool.wait_ge(S["fc2"], E_MLP)
            pool.memset(w1, 0.0).then_inc(S["ztile"], 1)
            pool.wait_ge(S["yo_out"], ONE + 16 * E_MLP)
            with pool.Fori(0, BH - 1) as k:
                sequence(k + BH, gather, k, False)
            sequence(B - 1, gather, BH - 1, True)

        @block.scalar
        def _(act):
            act.wait_ge(S["stat_d"], 1)
            act.activation(rstd, s4, ACT.Sqrt).then_inc(S["stat_a"], 1)
            act.wait_ge(S["stat_d"], 2)
            act.activation(r2, s5, ACT.Sqrt).then_inc(S["stat_a"], 1)
            act.wait_ge(S["init_rdy"], 1)
            act.wait_ge(S["const_rdy"], 4)

            def prologue(at):
                if at(3):
                    b, u, n = at(3)
                    act.wait_ge(S["dir_rdy"], n + 1)
                    wait_done(act, "hat_rdy", n)
                    act.copy(hat1[:], ps_p[:, 0, :]).then_inc(S["hat1_rdy"], 1)
                if at(6):
                    b, u, n = at(6)
                    act.wait_ge(S["u_rdy"], n + 1)
                    wait_done(act, "shift_rdy", n)
                    act.mul(ub[:], ps_u, -1.0).then_inc(S["ub_rdy"], 1)
                if at(1):
                    b, u, n = at(1)
                    act.wait_ge(S["qk_rdy"], n + 1)
                    wait_done(act, "rem_rdy", n - 1)
                    act.activation(v32[0:PROWS, u, :], ps_qk[0:PROWS, :], ACT.Identity, bias=bqk[0:PROWS, 0:1],
                                   scale=cst[0:PROWS, C_SCALE:C_SCALE + 1]).then_inc(S["v_rdy"], 1)
                    act.wait_ge(S["v_rdy"], n + 1)
                    wait_done(act, f"parts_out{u}", 64 * b)
                    wait_done(act, "dir_rdy", n - 1)
                    act.copy(parts[0:PROWS, u, 0, :], v32[0:PROWS, u, :]).then_inc(S["hi_rdy"], 1)
                    act.wait_ge(S["proj_rdy"], n + 1)
                    for half in range(2):
                        last = act.mul(va[:, bass.ds(b * TB + u * GT + 2 * half, 2), :, 0:DV],
                                       ps_v[:, half, :].rearrange("p (t c) -> p t c", t=2)[:, :, 0:C]
                                       .rearrange("p t (h d) -> p t h d", h=H), gam[:, 0:1])
                    last.then_inc(S["v_evac"], 1)
                if at(0):
                    b, u, n = at(0)
                    act.wait_ge(S["tr_rdy"], n + 1)
                    wait_done(act, "proj_rdy", n - 1)
                    act.copy(xnt[:, u, :], ps_t).then_inc(S["xnt_rdy"], 1)
                if at(1):
                    b, u, n = at(1)
                    act.wait_ge(S["rem_rdy"], n + 1)
                    act.copy(parts[0:PROWS, u, 1, :], rem[0:PROWS, u, :]).then_inc(S["mid_rdy"], 1)

            def expert_exponentials():
                act.wait_ge(S["off_rdy"], 1)
                act.activation(ex, lg_off, ACT.Exp).then_inc(S["r_exp"], 1)

            groups(act, prologue, {0: expert_exponentials})
            act.wait_ge(S["gate_rdy"], 1)

            def evacuate(b, hg, half):
                act.wait_ge(S["pv"], PV0 + NU * b + NS * hg + NS - 4 + 2 * (half + 1))
                if not (isinstance(b, int) and NHG * b + hg < 1):
                    act.wait_ge(S["o_rdy"], NHG * b + hg)
                act.copy(ot[:, half * HALF:(half + 1) * HALF], ps_acc[:, half, :]).then_inc(S["acc_evac"], 1)

            def sequence(b, first):
                for n in range(NU):
                    kc, g = n // HG, n % HG
                    if n % NS in (2, 4) and not (first and n < NS):
                        evacuate(b - (n < NS), (n // NS + 1) % NHG, n % NS // 2 - 1)
                    if isinstance(b, int) and b == 0 and n == 2 * HG - 1:
                        act.wait_ge(S["route"], 1)
                    if isinstance(b, int) and b == BH and n == 2 * HG - 1:
                        act.wait_ge(S["yo_out"], ONE + 16 * E_MLP)
                    for half in range(2):
                        act.wait_ge(S["s2"], 2 * (NU * b + n) + 1 + half)
                        if g == 0:
                            act.wait_ge(S["pv"], PV0 + NU * b + HG * (kc - 1) - 2 * (1 - half))
                        act.activation(pr[:, kc % 2, g, half * HALF:(half + 1) * HALF],
                                       ring[unit_job(n) % RING][:, half, :], ACT.Exp, scale=SLOPE
                                       ).then_inc(S["exps"], 1)

            def attention(b0):
                sequence(b0, True)
                with act.Fori(b0 + 1, b0 + BH) as b:
                    sequence(b, False)
                for half in range(2):
                    evacuate(b0 + BH - 1, NHG - 1, half)

            attention(0)

            def take_turned(e):
                for half in range(2):
                    act.wait_ge(S["etr"], 2 * e + half + 1)
                    act.copy(dt_[:, half * HALF:(half + 1) * HALF], ps[:, half, :]).then_inc(S["edt"], 1)

            def expert(e, u, last):
                for n in range(2 * FC):
                    half, f = n // FC, n % FC
                    act.wait_ge(S["fc1"], 2 * FC * e + n + 1)
                    act.activation(hs[:, f, half * HALF:(half + 1) * HALF], ps[:, 2 + n % 4, :], ACT.Gelu,
                                   bias=b1s[:, u, f:f + 1]).then_inc(S["gel"], 1)
                if not last:
                    take_turned(e + 1)

            take_turned(0)
            with act.Fori(0, E_MLP // 2 - 1) as k:
                for u in range(2):
                    expert(2 * k + u, u, False)
            for u in range(2):
                expert(E_MLP - 2 + u, u, u == 1)
            attention(BH)

        @block.tensor
        def _(pe):
            pe.sem_inc(S["pv"], PV0)
            pe.wait_ge(S["const_rdy"], 4)
            pe.wait_ge(S["init_rdy"], 1)

            def prologue(at):
                if at(1):
                    b, u, n = at(1)
                    pe.wait_ge(S["xnt_rdy"], n + 1)
                    wait_done(pe, "v_rdy", n)
                    pe.matmul(ps_qk[0:PROWS, :], wqk[:], xnt[:, u, :], start=True, stop=True).then_inc(S["qk_rdy"], 1)
                    wait_done(pe, "v_evac", n)
                    wait_done(pe, "lg_rdy", n)
                    for t in range(GT):
                        last = pe.matmul(ps_v[:, t // 2, (t % 2) * 256:(t % 2) * 256 + C + E],
                                         xnt[:, u, t * P:(t + 1) * P], wvr[:], start=True, stop=True)
                    last.then_inc(S["proj_rdy"], 1)
                if at(0):
                    b, u, n = at(0)
                    pe.wait_ge(S["xn_rdy"], n + 1)
                    wait_done(pe, "xnt_rdy", n)
                    for t in range(GT):
                        last = pe.transpose(ps_t[:, t * P:(t + 1) * P], xs[:, u, t, :], ident)
                    last.then_inc(S["tr_rdy"], 1)
                if at(2):
                    b, u, n = at(2)
                    pe.wait_ge(S["hi_rdy"], n + 1)
                    wait_done(pe, "ext_rdy", n)
                    wait_done(pe, "hat_rdy", n)
                    for o, col in ((ps_ku, C_KDIR), (ps_p[:, 0, :], C_PDIR), (ps_p[:, 1, :], C_RDIR)):
                        last = pe.matmul(o, cbf[0:PROWS, col:col + P], parts[0:PROWS, u, 0, :], start=True, stop=True)
                    last.then_inc(S["dir_rdy"], 1)
                if at(5):
                    b, u, n = at(5)
                    pe.wait_ge(S["hatm_rdy"], n + 1)
                    wait_done(pe, "shift_rdy", n)
                    pe.matmul(ps_u, cbf[:, C_BO:C_BO + H], hatm[:, u, :], start=True, stop=True
                              ).then_inc(S["u_rdy"], 1)

            groups(pe, prologue)
            for n, (lhs, rhs) in enumerate(((cbf[:, C_TRI:C_TRI + P], cnt), (onesb[:], incl))):
                pe.wait_ge(S["cnt_rdy"], n + 1)
                for half in range(2):
                    last = pe.matmul(ps_acc[:, half, :], lhs, rhs[:, half * HALF:(half + 1) * HALF], start=(n == 0),
                                     stop=(n == 1))
            last.then_inc(S["pos_rdy"], 1)
            def slot(b, j, half):
                before, jj = (b, j - RING) if j >= RING else (b - 1, NJ + j - RING)
                if not (isinstance(before, int) and before < 0):
                    if jj in UNIT_AT:
                        pe.wait_ge(S["exps"], 2 * (NU * before + UNIT_AT[jj]) + 1 + half)
                    elif jj > NJ // NHG:
                        pe.wait_ge(S["att_rdy"], NHG * before + 1)
                    elif not (isinstance(before, int) and before < 1):
                        pe.wait_ge(S["att_rdy"], NHG * before)
                return ring[j % RING][:, half, :]

            def scores(b, n):
                hg, kc, g = n // NS, n % NS // HG, n % HG
                if n % NS == 0:
                    pe.wait_ge(S[f"ld{hg}"], NLOAD * (b + 1))
                for half in range(2):
                    pe.matmul(slot(b, unit_job(n), half), kz[:, hg, g, kc * P:(kc + 1) * P],
                              q1[:, hg, half * HALF:(half + 1) * HALF], start=True, stop=True).then_inc(S["s1"], 1)

            def shifted(b, n):
                hg, kc, g = n // NS, n % NS // HG, n % HG
                for half in range(2):
                    pe.wait_ge(S["relu"], 2 * (NU * b + n) + 1 + half)
                    pe.matmul(ring[unit_job(n) % RING][:, half, :], kz[:, hg, g, kc * P:(kc + 1) * P],
                              q2[:, hg, half * HALF:(half + 1) * HALF], start=False, stop=True,
                              skip_group_check=True).then_inc(S["s2"], 1)

            def values(b, n):
                c, half = n // HG, n % HG // 2
                hg, kc = c // TB, c % TB
                if n % 2:
                    return
                if half == 0:
                    pe.wait_ge(S["exps"], 2 * (NU * b + HG * (c + 1)))
                if kc == 0:
                    if isinstance(b, int) and b == 0 and n == 0:
                        pe.wait_ge(S["gate_rdy"], 1)
                    if isinstance(b, int) and b == BH and n == 0:
                        pe.wait_ge(S["yo_rdy"], ONE + E_MLP)
                    pe.wait_ge(S["vp_rdy"], NHG * b + hg + 1)
                    wait_done(pe, "acc_evac", 2 * NHG * b + 2 * hg - 1 + half)
                for g in range(HG):
                    last = pe.matmul(ps_acc[32 * g:32 * g + 32, half, :], vp[:, hg, kc, g, :],
                                     pr[:, c % 2, g, half * HALF:(half + 1) * HALF],
                                     start=(kc == 0), stop=(kc == TB - 1), tile_position=(0, 32 * g))
                last.then_inc(S["pv"], 2)

            def turn(b, hg, slot_of):
                pe.wait_ge(S["acc_evac"], 2 * (NHG * b + hg + 1))
                for t in range(TB):
                    if t % GT == 0:
                        s = slot_of(t // GT)
                    last = pe.transpose(s[:, (t % GT) * P:(t % GT + 1) * P], ot[:, t * P:(t + 1) * P], ident)
                last.then_inc(S["o_rdy"], 1)

            def sequence(b, first, last):
                for n in range(NU):
                    if n + 1 == TURN and not first:
                        turn(b - 1, 1, lambda half: slot(b, unit_job(TURN) - 1, half))
                    if n + 1 == NS + TURN:
                        turn(b, 0, lambda half: slot(b, unit_job(NS + TURN) - 1, half))
                    if n + 1 < NU:
                        scores(b, n + 1)
                    elif not last:
                        scores(b + 1, 0)
                    if n >= VLAG:
                        values(b, n - VLAG)
                    elif not first:
                        values(b - 1, NU + n - VLAG)
                    shifted(b, n)

            def attention(b0):
                scores(b0, 0)
                sequence(b0, True, False)
                with pe.Fori(b0 + 1, b0 + BH - 1) as b:
                    sequence(b, False, False)
                end = b0 + BH - 1
                sequence(end, False, True)
                for n in range(NU - VLAG, NU):
                    values(end, n)
                turn(end, 1, lambda half: ring[TURN % RING][:, half, :])

            attention(0)

            def turn_rows(e, u):
                pe.wait_ge(S[f"ed{u}"], 40 * (e - u) + 80)
                wait_done(pe, "edt", 2 * e)
                for half in range(2):
                    for t in range(4):
                        j = half * 4 + t
                        last = pe.transpose(ps[:, half, t * P:(t + 1) * P], dd[u][:, j * P:(j + 1) * P], ident)
                    last.then_inc(S["etr"], 1)

            def expert(e, u, last):
                pe.wait_ge(S["edt"], 2 * (e + 1))
                for n in range(2 * FC):
                    half, f = n // FC, n % FC
                    pe.wait_ge(S["gel"], ONE + 2 * FC * e + max(n - 3, 0))
                    if n == 2:
                        pe.wait_ge(S["att_rdy"], NHG * BH)
                    pe.matmul(ps[:, 2 + n % 4, :], w1[:, 2 * u * FFN + f * P:2 * u * FFN + (f + 1) * P],
                              dt_[:, half * HALF:(half + 1) * HALF], start=True, stop=True).then_inc(S["fc1"], 1)
                pe.wait_ge(S["yo_rdy"], ONE + e)
                for half in range(2):
                    pe.wait_ge(S["gel"], ONE + 2 * FC * e + FC * (half + 1))
                    for j in range(half * ST // 2, (half + 1) * ST // 2):
                        o = ps[:, 6 + j // 4, (j % 4) * P:(j % 4 + 1) * P]
                        for f in range(FC):
                            mm = pe.matmul(o, hs[:, f, j * P:(j + 1) * P],
                                           w1[:, (2 * u + 1) * FFN + f * P:(2 * u + 1) * FFN + (f + 1) * P],
                                           start=(f == 0), stop=(f == FC - 1))
                    if half == 0 and not last:
                        turn_rows(e + 1, 1 - u)
                mm.then_inc(S["fc2"], 1)

            turn_rows(0, 0)
            with pe.Fori(0, E_MLP // 2 - 1) as k:
                for u in range(2):
                    expert(2 * k + u, u, False)
            for u in range(2):
                expert(E_MLP - 2 + u, u, u == 1)
            pe.wait_ge(S["gel"], ONE + 8 * E_MLP)
            attention(BH)

        @block.vector
        def _(dve):
            step = [0]
            stat = S["bns"]

            def link(ins):
                step[0] += 1
                ins.then_inc(stat, 1)
                dve.wait_ge(stat, step[0])

            for name in FROM_ONE:
                dve.sem_inc(S[name], ONE)
            dve.sem_inc(S["comb"], CO0)
            for b in range(B):
                dve.wait_ge(S[f"x_in{b}"], 16)
                for t in range(TB):
                    last = dve.bn_stats(bst[:, b * TB + t, :], y[:, b * TB + t, :])
            link(last)
            dve.wait_ge(S["w_in"], 16 * 10)
            dve.tensor_copy(cbf[:], cst[:, 0:C_SCALE]).then_inc(S["const_rdy"], 1)
            dve.tensor_scalar(wvr[:, C:C + E], wvr[:, C:C + E], nw[:, 0:1], None, ALU.mult
                              ).then_inc(S["const_rdy"], 1)
            dve.tensor_scalar(bqk[0:PROWS, :], bqk[0:PROWS, :], cst[0:PROWS, C_SCALE:C_SCALE + 1], None, ALU.mult
                              ).then_inc(S["const_rdy"], 1)
            dve.tensor_scalar(bvg[:], bvg[:], gam[:, 0:1], None, ALU.mult).then_inc(S["const_rdy"], 1)
            me, se, mo, so = (bst[:, :, k] for k in (1, 2, 4, 5))
            link(dve.tensor_tensor(mean, me, mo, ALU.add))
            link(dve.tensor_tensor(s6, me, mo, ALU.subtract))
            link(dve.tensor_tensor(var, se, so, ALU.add))
            link(dve.tensor_tensor(s6, s6, s6, ALU.mult))
            link(dve.tensor_scalar(mean, mean, 0.5, None, ALU.mult))
            link(dve.tensor_scalar(var, var, 1.0 / C, None, ALU.mult))
            link(dve.scalar_tensor_tensor(out=var, in0=s6, scalar=0.25, in1=var, op0=ALU.mult, op1=ALU.add))
            dve.tensor_scalar(s4, var, EPS, None, ALU.add).then_inc(S["stat_d"], 1)
            dve.wait_ge(S["stat_a"], 1)
            link(dve.reciprocal(rstd, rstd))
            link(dve.tensor_tensor(s7, var, rstd, ALU.mult))
            link(dve.tensor_tensor(s7, s7, rstd, ALU.mult))
            dve.tensor_scalar(s5, s7, EPS, None, ALU.add).then_inc(S["stat_d"], 1)
            dve.wait_ge(S["stat_a"], 2)
            dve.reciprocal(r2, r2).then_inc(S["stat_rdy"], 1)
            dve.wait_ge(S["stat_rdy"], 1)

            def prologue(at):
                if at(0):
                    b, u, n = at(0)
                    wait_done(dve, "tr_rdy", n - 1)
                    wait_done(dve, "y_upd", n - 1)
                    wait_done(dve, "xn2_rdy", n - 1)
                    for t in range(GT):
                        tt = bass.ds(b * TB + u * GT + t, 1)
                        last = dve.tensor_scalar(xs[:, u, t, :], y[:, tt, :].rearrange("p a c -> p (a c)"),
                                                 mean[:, tt], rstd[:, tt], ALU.subtract, ALU.mult)
                    last.then_inc(S["xn_rdy"], 1)
                if at(3):
                    b, u, n = at(3)
                    dve.wait_ge(S["dir_rdy"], n + 1)
                    wait_done(dve, "kmax_rdy", b)
                    dve.tensor_reduce(kmax2[:, u:u + 1], ps_ku, AX.X, ALU.max).then_inc(S["ext_rdy"], 1)
                    if u == 1:
                        dve.wait_ge(S["ext_rdy"], n + 1)
                        wait_done(dve, "hatm_rdy", 2 * b)
                        dve.tensor_tensor(kmax[:], kmax2[:, 0:1], kmax2[:, 1:2], ALU.max).then_inc(S["kmax_rdy"], 1)
                    dve.wait_ge(S["hat1_rdy"], n + 1)
                    wait_done(dve, "hatm_rdy", n - 1)
                    dve.tensor_tensor(hat[:, u, :], ps_p[:, 1, :], hat1[:], ALU.min).then_inc(S["hat_rdy"], 1)
                if at(4):
                    b, u, n = at(4)
                    dve.wait_ge(S["hat_rdy"], n + 1)
                    dve.wait_ge(S["kmax_rdy"], b + 1)
                    wait_done(dve, "u_rdy", n - 1)
                    dve.tensor_scalar(hatm[:, u, :], hat[:, u, :], 0.0, kmax[:, 0:1], ALU.max, ALU.mult
                                      ).then_inc(S["hatm_rdy"], 1)
                if at(6):
                    b, u, n = at(6)
                    dve.wait_ge(S["ub_rdy"], n + 1)
                    wait_done(dve, f"shift_out{u}", 16 * b)
                    dve.scalar_tensor_tensor(out=shift[:, u, :], in0=ps_u, scalar=-1.0 / SLOPE, in1=ub[:],
                                             op0=ALU.mult, op1=ALU.min).then_inc(S["shift_rdy"], 1)
                if at(1):
                    b, u, n = at(1)
                    tiles = bass.ds(b * TB + u * GT, GT)
                    dve.wait_ge(S["proj_rdy"], n + 1)
                    dve.wait_ge(S["v_evac"], n + 1)
                    dve.tensor_tensor(lg[:, tiles, :].rearrange("p (a t) e -> p a t e", a=2),
                                      ps_v.rearrange("p a (t c) -> p a t c", t=2)[:, :, :, C:C + E],
                                      r2[:, tiles].rearrange("p (a t) -> p a t", a=2).unsqueeze(3)
                                      .broadcast_to([P, 2, 2, E]), ALU.mult).then_inc(S["lg_rdy"], 1)
                if at(0):
                    b, u, n = at(0)
                    dve.wait_ge(S["xn_rdy"], n + 1)
                    for t in range(GT):
                        tt = bass.ds(b * TB + u * GT + t, 1)
                        last = dve.scalar_tensor_tensor(out=xn2[:, tt, :].rearrange("p a c -> p (a c)"),
                                                        in0=xs[:, u, t, :], scalar=r2[:, tt], in1=nwr[:],
                                                        op0=ALU.mult, op1=ALU.mult)
                    last.then_inc(S["xn2_rdy"], 1)

            def tiles_of(v):
                return v.rearrange("p (t e) -> p t e", e=E)

            def per_tile(v):
                return v.unsqueeze(2).broadcast_to([P, NT, E])

            onehot = oh1, oh2
            descb = cbf[:, C_DESC:C_DESC + E].unsqueeze(1).broadcast_to([P, NT, E])

            def first_of_equals(k, value, largest):
                link(dve.tensor_tensor(tiles_of(rank_of), value, per_tile(largest), ALU.is_equal))
                link(dve.tensor_tensor(tiles_of(rank_of), tiles_of(rank_of), descb, ALU.mult))
                link(dve.tensor_reduce(rank[:, k, :], tiles_of(rank_of), AX.X, ALU.max))
                link(dve.tensor_copy(rank_b[:, k, :], rank[:, k, :]))
                link(dve.tensor_tensor(tiles_of(onehot[k]), tiles_of(rank_of), per_tile(rank_b[:, k, :]), ALU.is_equal))

            def first_choice():
                dve.wait_ge(S["zero_in"], 16 * E_MLP)
                dve.wait_ge(S["lg_rdy"], 2 * B)
                link(dve.tensor_tensor(lg[:], lg[:], rb[:].unsqueeze(1).broadcast_to([P, NT, E]), ALU.add))
                dve.tensor_reduce(top, lg[:], AX.X, ALU.max).then_inc(S["max_rdy"], 1)
                dve.wait_ge(S["max_rdy"], 1)
                first_of_equals(0, lg[:], top)

            def second_value():
                dve.wait_ge(S["r_exp"], 1)
                link(dve.tensor_reduce(total, tiles_of(ex), AX.X, ALU.add))
                link(dve.reciprocal(gate[:, 0, :], total))
                link(dve.scalar_tensor_tensor(out=ex, in0=oh1, scalar=-2.0, in1=ex, op0=ALU.mult, op1=ALU.add))
                link(dve.tensor_reduce(inv, tiles_of(ex), AX.X, ALU.max))
                link(dve.tensor_tensor(gate[:, 1, :], inv, gate[:, 0, :], ALU.mult))

            def second_choice():
                first_of_equals(1, tiles_of(ex), inv)

            groups(dve, prologue, {0: first_choice, 2: second_value, 3: second_choice})
            dve.tensor_tensor(cnt.rearrange("p (e t) -> p t e", t=NT), tiles_of(oh1), tiles_of(oh2), ALU.add
                              ).then_inc(S["cnt_rdy"], 1)
            dve.wait_ge(S["cnt_rdy"], 1)
            dve.wait_ge(S["reset_rdy"], 1)
            dve.tensor_tensor_scan(incl, reset, cnt, 0.0, ALU.mult, ALU.add).then_inc(S["cnt_rdy"], 1)
            dve.wait_ge(S["pos_rdy"], 1)
            pos = ps_acc.rearrange("p a m -> p (a m)").rearrange("p (e t) -> p t e", t=NT)
            for k in range(2):
                dve.tensor_tensor(tiles_of(prod[k]), pos, tiles_of(onehot[k]), ALU.mult).then_inc(stat, 1)
                step[0] += 1
            dve.wait_ge(stat, step[0])
            for k in range(2):
                last = dve.tensor_reduce(at[:, k, :], tiles_of(prod[k]), AX.X, ALU.add)
            link(last)
            link(dve.tensor_scalar(keep, at, float(CAP), None, ALU.is_lt))
            link(dve.tensor_tensor(gate, gate, keep, ALU.mult))
            link(dve.tensor_tensor(total, gate[:, 0, :], gate[:, 1, :], ALU.add))
            link(dve.tensor_scalar(inv, total, 0.0, None, ALU.is_le))
            link(dve.tensor_tensor(total2, total, inv, ALU.add))
            link(dve.reciprocal(inv, total2))
            dve.tensor_tensor(gate, gate, inv.unsqueeze(1).broadcast_to([P, 2, NT]), ALU.mult).then_inc(S["gate_rdy"], 1)


            def denominators(b, hg, j):
                dve.wait_ge(S["o_rdy"], NHG * b + hg + 1)
                dve.reciprocal(rg[:], turned(j)[:, :, :, DV]).then_inc(S["rg_rdy"], 1)

            def finish(b, hg, j):
                m = NHG * b + hg
                dve.wait_ge(S["rg_rdy"], m + 1)
                wait_done(dve, "y_att", m)
                dve.tensor_tensor(att[:], turned(j)[:, :, :, 0:DV], rg[:].unsqueeze(3).broadcast_to([P, TB, HG, DV]),
                                  ALU.mult).then_inc(S["att_rdy"], 1)

            def turned(j):
                return ring[j % RING].rearrange("p a (t g c) -> p (a t) g c", g=HG, c=32)

            def sequence(b, first):
                for n in range(NU):
                    if n == TURN and not first:
                        denominators(b - 1, 1, unit_job(TURN) - 1)
                    if n == NS + TURN:
                        denominators(b, 0, unit_job(NS + TURN) - 1)
                    for half in range(2):
                        dve.wait_ge(S["s1"], 2 * (NU * b + n) + 1 + half)
                        s = ring[unit_job(n) % RING][:, half, :]
                        dve.tensor_scalar(s, s, 0.0, 1.0 / SLOPE - 1.0, ALU.max, ALU.mult).then_inc(S["relu"], 1)
                    if n == TURN and not first:
                        finish(b - 1, 1, unit_job(TURN) - 1)
                    if n == NS + TURN:
                        finish(b, 0, unit_job(NS + TURN) - 1)

            sequence(0, True)
            with dve.Fori(1, BH) as b:
                sequence(b, False)
            denominators(BH - 1, 1, TURN)
            finish(BH - 1, 1, TURN)

            with dve.Fori(0, E_MLP // 2) as k:
                for u in range(2):
                    e = 2 * k + u
                    dve.wait_ge(S["fc2"], e + 1)
                    dve.wait_ge(S["yo_out"], ONE + 16 * e)
                    dve.tensor_tensor(yo.rearrange("p (j c) -> p j c", c=C),
                                      ps[:, 6:8, :].rearrange("p a (j c) -> p (a j) c", c=C),
                                      b2s[:, u, :].unsqueeze(1).broadcast_to([P, ST, C]), ALU.add
                                      ).then_inc(S["yo_rdy"], 1)
            sequence(BH, True)
            with dve.Fori(BH + 1, B) as b:
                sequence(b, False)
            denominators(B - 1, 1, TURN)
            finish(B - 1, 1, TURN)


_INS = ("x", "consts", "w_qk", "b_qk", "w_vr", "b_v", "r_b", "n_w", "n_w_row", "w1t", "b1", "w2t", "b2", "cvec",
        "gamma")


def layouts(i):
    import numpy as np

    a = {k.split("_", 1)[1]: np.asarray(v) for k, v in i.items()}
    q, k = ({n: a[f"attn_{n}{w}"].reshape(H, DQ, -1).transpose(1, 0, 2).reshape(QP, -1) for n in "Wb"} for w in "qk")
    rows = {}
    for n, width in (("W", C), ("b", 1)):
        r = np.zeros((PROWS, width), np.float32)
        r[0:3 * QP] = np.tile(q[n], (3, 1))
        r[KROW:] = np.tile(k[n], (3, 1))
        rows[n] = r
    return {
        "x": a["attn_x"].reshape(T, C),
        "consts": constants(),
        "w_qk": rows["W"].T,
        "b_qk": rows["b"],
        "w_vr": np.concatenate([a["attn_Wv"].T, a["ffn_router_weight"].T], axis=1),
        "b_v": a["attn_bv"].reshape(1, C),
        "r_b": a["ffn_router_bias"].reshape(1, E),
        "n_w": a["ffn_norm_weight"].reshape(C, 1),
        "n_w_row": a["ffn_norm_weight"].reshape(1, C),
        "w1t": a["ffn_fc1_weight"].transpose(0, 2, 1),
        "b1": a["ffn_fc1_bias"].reshape(E_MLP, FC, P).transpose(0, 2, 1),
        "w2t": a["ffn_fc2_weight"].transpose(0, 2, 1).reshape(E_MLP, FC, P, C).transpose(0, 2, 1, 3).reshape(E_MLP, P, FC * C),
        "b2": a["ffn_fc2_bias"],
        "cvec": a["ffn_constant_vectors"].reshape(1, 2, C),
        "gamma": a["attn_gamma"].reshape(1, 1),
    }


def kernel(**inputs):
    import numpy as np
    import concourse.bacc as bacc
    from concourse.bass_utils import run_bass_kernel_spmd

    nc = bacc.Bacc("TRN2", target_bir_lowering=False, num_devices=1)
    arrays, args = {}, []
    laid = layouts(inputs)
    for name in _INS:
        v = np.ascontiguousarray(laid[name])
        arrays[f"in_{name}"] = v
        args.append(nc.dram_tensor(f"in_{name}", v.shape, mybir.dt.from_np(v.dtype), kind="ExternalInput").ap())
    out = nc.dram_tensor("out", [T, C], F32, kind="ExternalOutput").ap()
    build(nc, *args, out)
    r = run_bass_kernel_spmd(nc, [arrays], core_ids=[0])
    return r.results[0]["out"].reshape(B, M, C)
```
